# Optimizing a Trainium2 kernel written in Bass

```python
import numpy as np
import jax
import jax.numpy as jnp

def _softmax(x, axis=-1):
    return jax.nn.softmax(x, axis=axis)

def _gelu(x):
    return jax.nn.gelu(x, approximate=True)

def _silu(x):
    return jax.nn.silu(x)

def _sigmoid(x):
    return jax.nn.sigmoid(x)

def _layernorm(x, axis=-1, eps=1e-05):
    m = jnp.mean(x, axis=axis, keepdims=True)
    v = jnp.var(x, axis=axis, keepdims=True)
    return (x - m) / jnp.sqrt(v + eps)

def _scatter_add(tgt, idx, src, axis=0):
    return tgt.at[idx].add(src)

def _segment_sum(src, seg, n):
    return jax.ops.segment_sum(src, seg, n)
kernel_name = 'mk_gps_d1_gnn_r8_7035f7'

def setup_inputs(seed: int=0):
    np.random.seed(seed)
    _w = jnp.asarray

    def _rec_inputs():
        import jax
        import jax.numpy as jnp
        _gk = jax.random.key(seed)
        x = 1.271e-05 + 0.05 * jax.random.normal(jax.random.fold_in(_gk, 1), (6250, 256), jnp.float32)
        src = jax.random.randint(jax.random.fold_in(_gk, 2), (100000,), 0, 6250, jnp.int32)
        dst = jax.random.randint(jax.random.fold_in(_gk, 3), (100000,), 0, 6250, jnp.int32)
        _o = jnp.argsort(dst, stable=True)
        src = src[_o]
        dst = dst[_o]
        edge_type_8 = jax.random.randint(jax.random.fold_in(_gk, 12), (100000,), 0, 8, jnp.int32)
        return (x, src, dst, edge_type_8)
    x, src, dst, edge_type_8 = _rec_inputs()

    def _L0_gnn_setup():
        import jax, jax.numpy as jnp
        import numpy as np
        N_NODES = 6250
        N_EDGES = 100000
        N_REL = 8
        HID = 256
        N_BASES = 30
        N_LAYERS = 2
        key = jax.random.key(seed)
        ks = jax.random.split(key, 6)
        edge_index = jax.random.randint(ks[0], (2, N_EDGES), 0, N_NODES)
        edge_type = jax.random.randint(ks[1], (N_EDGES,), 0, N_REL)
        s_w = (6.0 / (HID + HID)) ** 0.5
        emb = jax.random.normal(ks[2], (N_NODES, HID), dtype=jnp.float32) * 0.05
        bases = jax.random.uniform(ks[3], (N_LAYERS, N_BASES, HID, HID), dtype=jnp.float32, minval=-s_w, maxval=s_w)
        coeffs = jax.random.uniform(ks[4], (N_LAYERS, N_REL, N_BASES), dtype=jnp.float32, minval=-0.4, maxval=0.4)
        self_loops = jax.random.uniform(ks[5], (N_LAYERS, HID, HID), dtype=jnp.float32, minval=-s_w, maxval=s_w)
        return {'edge_index': edge_index, 'edge_type': edge_type, 'num_nodes': N_NODES, 'emb': emb, 'bases': bases, 'coeffs': coeffs, 'self_loops': self_loops}
    _L0_gnn_all = _L0_gnn_setup()
    _L0_gnn_in = {k: v for k, v in _L0_gnn_all.items() if k in ('bases', 'coeffs', 'self_loops')}
    del _L0_gnn_all

    def _L0_mix_setup():
        import jax, jax.numpy as jnp
        import numpy as np
        D_MODEL = 256
        NUM_HEADS = 8
        DEPTH = D_MODEL // NUM_HEADS
        B, L = (32, 512)

        def _feature_map(x):
            return jax.nn.elu(x) + 1.0
        key = jax.random.key(seed)
        ks = jax.random.split(key, 9)
        sc = 1.0 / np.sqrt(D_MODEL)
        return {'x': jax.random.normal(ks[0], (B, L, D_MODEL), dtype=jnp.float32), 'wq': jax.random.normal(ks[1], (D_MODEL, D_MODEL), dtype=jnp.float32) * sc, 'bq': jnp.zeros((D_MODEL,), dtype=jnp.float32), 'wk': jax.random.normal(ks[2], (D_MODEL, D_MODEL), dtype=jnp.float32) * sc, 'bk': jnp.zeros((D_MODEL,), dtype=jnp.float32), 'wv': jax.random.normal(ks[3], (D_MODEL, D_MODEL), dtype=jnp.float32) * sc, 'bv': jnp.zeros((D_MODEL,), dtype=jnp.float32), 'wo': jax.random.normal(ks[4], (D_MODEL, D_MODEL), dtype=jnp.float32) * sc, 'bo': jnp.zeros((D_MODEL,), dtype=jnp.float32)}
    _L0_mix_all = _L0_mix_setup()
    _L0_mix_in = {k: v for k, v in _L0_mix_all.items() if k in ('wq', 'bq', 'wk', 'bk', 'wv', 'bv', 'wo', 'bo')}
    del _L0_mix_all

    def _L0_ffn_setup():
        import jax, jax.numpy as jnp
        import numpy as np
        B, K, D = (512, 16, 256)
        E = 32
        H = int(D * 0.25)
        key = jax.random.key(seed)
        ks = jax.random.split(key, 7)
        d_rs = D ** (-0.5)
        h_rs = H ** (-0.5)
        x = jax.random.normal(ks[0], (B, K, D), dtype=jnp.float32)
        router_w = jax.random.uniform(ks[1], (E, D), jnp.float32, -d_rs, d_rs)
        router_b = jax.random.uniform(ks[2], (E,), jnp.float32, -d_rs, d_rs)
        W1 = jax.random.uniform(ks[3], (E, D, H), jnp.float32, -h_rs, h_rs)
        b1 = jax.random.uniform(ks[4], (E, H), jnp.float32, -h_rs, h_rs)
        W2 = jax.random.uniform(ks[5], (E, H, D), jnp.float32, -d_rs, d_rs)
        b2 = jax.random.uniform(ks[6], (E, D), jnp.float32, -d_rs, d_rs)
        return {'x': x, 'router_w': router_w, 'router_b': router_b, 'W1': W1, 'b1': b1, 'W2': W2, 'b2': b2}
    _L0_ffn_all = _L0_ffn_setup()
    _L0_ffn_in = {k: v for k, v in _L0_ffn_all.items() if k in ('router_w', 'router_b', 'W1', 'b1', 'W2', 'b2')}
    del _L0_ffn_all
    return {'x': x, 'src': src, 'dst': dst, 'edge_type_8': edge_type_8, 'L0_gnn_bases': _L0_gnn_in['bases'], 'L0_gnn_coeffs': _L0_gnn_in['coeffs'], 'L0_gnn_self_loops': _L0_gnn_in['self_loops'], 'L0_mix_wq': _L0_mix_in['wq'], 'L0_mix_bq': _L0_mix_in['bq'], 'L0_mix_wk': _L0_mix_in['wk'], 'L0_mix_bk': _L0_mix_in['bk'], 'L0_mix_wv': _L0_mix_in['wv'], 'L0_mix_bv': _L0_mix_in['bv'], 'L0_mix_wo': _L0_mix_in['wo'], 'L0_mix_bo': _L0_mix_in['bo'], 'L0_ffn_router_w': _L0_ffn_in['router_w'], 'L0_ffn_router_b': _L0_ffn_in['router_b'], 'L0_ffn_W1': _L0_ffn_in['W1'], 'L0_ffn_b1': _L0_ffn_in['b1'], 'L0_ffn_W2': _L0_ffn_in['W2'], 'L0_ffn_b2': _L0_ffn_in['b2']}

def reference(x, src, dst, edge_type_8, L0_gnn_bases, L0_gnn_coeffs, L0_gnn_self_loops, L0_mix_wq, L0_mix_bq, L0_mix_wk, L0_mix_bk, L0_mix_wv, L0_mix_bv, L0_mix_wo, L0_mix_bo, L0_ffn_router_w, L0_ffn_router_b, L0_ffn_W1, L0_ffn_b1, L0_ffn_W2, L0_ffn_b2):
    import jax
    import jax.numpy as jnp

    def _L0_gnn_ref(edge_index, edge_type, num_nodes, emb, bases, coeffs, self_loops):
        import jax, jax.numpy as jnp
        import numpy as np
        N_NODES = 6250
        N_EDGES = 100000
        N_REL = 8
        HID = 256
        N_BASES = 30
        N_LAYERS = 2
        src, dst = (edge_index[0], edge_index[1])
        deg = jax.ops.segment_sum(jnp.ones_like(dst, dtype=emb.dtype), dst, num_segments=num_nodes)
        deg_inv = 1.0 / jnp.maximum(deg, 1.0)
        x = emb
        n_layers = bases.shape[0]
        for l in range(n_layers):
            W = jnp.einsum('rb,bio->rio', coeffs[l], bases[l])
            h = jnp.einsum('ni,rio->rno', x, W)
            msg = h[edge_type, src] * deg_inv[dst][:, None]
            agg = jax.ops.segment_sum(msg, dst, num_segments=num_nodes)
            x_new = agg + x @ self_loops[l]
            if l < n_layers - 1:
                x_new = jax.nn.relu(x_new)
            x = x_new
        return x

    def _L0_mix_ref(x, wq, bq, wk, bk, wv, bv, wo, bo):
        import jax, jax.numpy as jnp
        import numpy as np
        D_MODEL = 256
        NUM_HEADS = 8
        DEPTH = D_MODEL // NUM_HEADS
        B, L = (32, 512)

        def _feature_map(x):
            return jax.nn.elu(x) + 1.0
        b, l, _ = x.shape
        q = (x @ wq + bq).reshape(b, l, NUM_HEADS, DEPTH)
        k = (x @ wk + bk).reshape(b, l, NUM_HEADS, DEPTH)
        v = (x @ wv + bv).reshape(b, l, NUM_HEADS, DEPTH)
        q = _feature_map(q)
        k = _feature_map(k)
        kv = jnp.einsum('blhd,blhe->bhde', k, v)
        k_sum = jnp.sum(k, axis=1)
        qkv = jnp.einsum('blhd,bhde->blhe', q, kv)
        normalizer = jnp.einsum('blhd,bhd->blh', q, k_sum) + 1e-06
        out = qkv / normalizer[..., None]
        out = out.reshape(b, l, D_MODEL)
        return out @ wo + bo

    def _L0_ffn_ref(x, router_w, router_b, W1, b1, W2, b2):
        import jax, jax.numpy as jnp
        import numpy as np
        B, K, D = (512, 16, 256)
        E = 32
        H = int(D * 0.25)
        xf = x.reshape(-1, D)
        logits = xf @ router_w.T + router_b
        idx = jnp.argmax(logits, axis=-1)
        w1t = jnp.take(W1, idx, axis=0)
        h = jnp.einsum('nd,ndh->nh', xf, w1t) + jnp.take(b1, idx, axis=0)
        h = jax.nn.relu(h)
        w2t = jnp.take(W2, idx, axis=0)
        out = jnp.einsum('nh,nhd->nd', h, w2t) + jnp.take(b2, idx, axis=0)
        out = jax.nn.relu(out)
        return out.reshape(x.shape)
    edge_index = jnp.stack([src, dst])
    xn = _layernorm(x, axis=-1)
    x = x + _L0_gnn_ref(edge_index, edge_type_8, 6250, xn, L0_gnn_bases, L0_gnn_coeffs, L0_gnn_self_loops) + _L0_mix_ref(xn[None], L0_mix_wq, L0_mix_bq, L0_mix_wk, L0_mix_bk, L0_mix_wv, L0_mix_bv, L0_mix_wo, L0_mix_bo)[0]
    x = x + _L0_ffn_ref(_layernorm(x, axis=-1)[None], L0_ffn_router_w, L0_ffn_router_b, L0_ffn_W1, L0_ffn_b1, L0_ffn_W2, L0_ffn_b2)[0]
    return x

_drawn_inputs = setup_inputs


def setup_inputs(seed=0):
    import zlib

    import numpy as np

    out = dict(_drawn_inputs(seed))
    spreads = {'L0_mix_bq': (0.0, 0.8),
     'L0_mix_bk': (0.0, 0.8),
     'L0_mix_bv': (0.0, 0.1),
     'L0_mix_bo': (0.0, 0.1)}
    factors = {'L0_mix_wq': 3.311, 'L0_ffn_b1': 4.27}
    for name, (base, spread) in spreads.items():
        noise = np.random.default_rng([zlib.crc32(name.encode()), seed]).standard_normal(out[name].shape)
        drawn = base * np.exp(spread * noise) if base else spread * noise
        out[name] = jnp.asarray(drawn.astype(out[name].dtype))
    for name, factor in factors.items():
        out[name] = (out[name] * factor).astype(out[name].dtype)
    return out
```

```python
from contextlib import ExitStack

import numpy as np

import concourse.bass as bass
from concourse import mybir

F32 = mybir.dt.float32
BF16 = mybir.dt.bfloat16
I32 = mybir.dt.int32
ALU = mybir.AluOpType
ACT = mybir.ActivationFunctionType
AX = mybir.AxisListType
ds = bass.ds

P = 128
N, D = 6250, 256
NB = -(-N // P)
NP = NB * P
LAST = N - (NB - 1) * P
H2 = D // P
NE = 100000
NT = -(-NE // P)
R = 8
NBASE = 30
WD = P // R
WPB = P // WD
NW = NB * WPB
RING = 16
GRP = 4
NTP = -(-NT // RING) * RING
RO = 16
NRE = (NTP - RING) // GRP
HD = 32
CH = 448
E, HID = 32, 64
NC = E * HID // P
BIG = 1e30
EPS = 1e-5
PAD_DST = 8 * N


def take(eng, sem, n=1):
    eng.wait_ge(sem, n)
    eng.sem_inc(sem, -n)


class Scope:

    def __init__(self, nc, ctx, tag):
        self.nc, self.ctx, self.tag = nc, ctx, tag

    def sb(self, name, shape, dt=F32):
        return self.ctx.enter_context(self.nc.sbuf_tensor(f"{self.tag}_{name}", shape, dt))

    def ps(self, name, shape, dt=F32):
        return self.ctx.enter_context(self.nc.psum_tensor(f"{self.tag}_{name}", shape, dt))

    def sem(self, name):
        return self.ctx.enter_context(self.nc.semaphore(f"{self.tag}_{name}"))


class Shared:

    def __init__(self, nc, ctx):
        s = Scope(nc, ctx, "g")
        self.xT = s.sb("xT", [P, H2, NP])
        self.key = s.sb("key", [P, NTP])
        self.idx = s.sb("idx", [P, NTP], I32)
        self.wbase = s.sb("wbase", [P, NW])
        self.bound = s.sb("bound", [1, 4 * P], I32)
        self.reuse = s.sb("reuse", [1, NRE], I32)
        self.iota = s.sb("iota", [P, P])
        self.ident = s.sb("ident", [P, P])
        self.zero = s.sb("zero", [P, P], BF16)
        self.ones = s.sb("ones", [P, P], BF16)
        self.one = s.sb("one", [1, 2])
        self.dinv = s.sb("dinv", [P, NB])
        dram = lambda name, shape, dt: nc.dram_tensor(name, shape, dt).ap()
        self.table = [dram(f"table{l}", (NP, 3 * D), BF16) for l in range(2)]
        self.wrel = dram("wrel", (2 * R, D * D), F32)
        self.bounds = dram("bounds", (4 * P,), I32)
        self.base = dram("base", (NP, D), F32)
        self.x2 = dram("x2", (NP, D), F32)


def prepare(nc, g, a):
    G = 7
    NG = NB // G
    IC = 8
    NS = D // 4 // IC
    with ExitStack() as ctx:
        s = Scope(nc, ctx, "pre")
        xs = s.sb("xs", [P, NB, D])
        sq = s.sb("sq", [P, G, D])
        xn = s.sb("xn", [P, G, D])
        st = s.sb("st", [P, 4, G])
        tb = s.sb("tb", [P, G, 3 * D], BF16)
        dsti = s.sb("dsti", [P, NTP], I32)
        eti = s.sb("eti", [P, NTP], I32)
        ka = s.sb("ka", [P, NTP], I32)
        kb = s.sb("kb", [P, NTP], I32)
        kc = s.sb("kc", [P, NTP])
        dl = s.sb("dl", [P, NT - 1], I32)
        before = s.sb("before", [P, NT - 1])
        w16i = s.sb("w16i", [P, 4], I32)
        w16 = s.sb("w16", [P, 4])
        bf = s.sb("bf", [P, 4])
        bi = s.sb("bi", [P, 4], I32)
        iti = s.sb("iti", [P, P], I32)
        wbi = s.sb("wbi", [P, NW], I32)
        uio = s.sb("uio", [1, NRE], I32)
        ush = s.sb("ush", [1, NRE], I32)
        idi = s.sb("idi", [P, P], I32)
        cf = s.sb("cf", [4 * NBASE, 2, 4 * R])
        bs = s.sb("bs", [4 * NBASE, 2, IC * D])
        wst = s.sb("wst", [4 * R, IC * D])
        pT = s.ps("pT", [P, G, H2 * P])
        pw = s.ps("pw", [4 * R, IC * D])

        x_in, x_pad, e_in, io, const_ok = (s.sem(n) for n in ("x_in", "x_pad", "e_in", "io", "const_ok"))
        dve_own, var_ok, std_ok, xn_ok = (s.sem(n) for n in ("dve_own", "var_ok", "std_ok", "xn_ok"))
        tb_ok, tb_out, xT_ps, xT_psfree = (s.sem(n) for n in ("tb_ok", "tb_out", "xT_ps", "xT_psfree"))
        bi_ok, bi_out, bound_in = (s.sem(n) for n in ("bi_ok", "bi_out", "bound_in"))
        cf_zero, cf_in, bs_free, w_ps, w_psfree = (s.sem(n) for n in ("cf_zero", "cf_in", "bs_free", "w_ps", "w_psfree"))
        xn_free = s.sem("xn_free")
        w_sb, w_out = s.sem("w_sb"), s.sem("w_out")
        bs_in = [s.sem(f"bs_in{k}") for k in range(2)]
        bases = [a["L0_gnn_bases"][l].rearrange("b (q i) o -> q b (i o)", q=4) for l in range(2)]

        block = ctx.enter_context(nc.Block())

        @block.sync
        def _(eng):
            eng.dma_start(xs[:, 0:NB - 1, :],
                          a["x"][0:(NB - 1) * P, :].rearrange("(b p) d -> p b d", p=P)).then_inc(x_in, 16)
            eng.wait_ge(x_pad, 1)
            eng.dma_start(xs[0:LAST, NB - 1, :], a["x"][(NB - 1) * P:N, :]).then_inc(x_in, 16)
            eng.dma_start(dsti[:, :], a["dst"]).then_inc(e_in, 16)
            eng.dma_start(eti[:, :], a["edge_type_8"]).then_inc(e_in, 16)
            eng.dma_start(g.idx[:, :], a["src"]).then_inc(e_in, 16)
            eng.dma_start(dl[:, :], a["dst"][P - 1:P, 0:NT - 1].to_broadcast([P, NT - 1])).then_inc(e_in, 16)
            eng.wait_ge(cf_zero, 1)
            for l in range(2):
                for q in range(4):
                    eng.dma_start(cf[q * NBASE:(q + 1) * NBASE, l, q * R:(q + 1) * R],
                                  a["L0_gnn_coeffs"][l]).then_inc(cf_in, 16)
            eng.wait_ge(bi_ok, 1)
            eng.dma_start(g.bounds.rearrange("(p c) -> p c", c=4), bi[:, :]).then_inc(bi_out, 16)
            eng.wait_ge(bi_out, 16)
            eng.dma_start(g.bound[:, :], g.bounds.rearrange("(a w) -> a w", a=1)).then_inc(bound_in, 16)
            for l in range(2):
                with eng.Fori(0, NS // 2) as c:
                    for k in range(2):
                        take(eng, bs_free)
                        for q in range(4):
                            eng.dma_start(bs[q * NBASE:(q + 1) * NBASE, k, :],
                                          bases[l][q, :, ds((c * 2 + k) * (IC * D), IC * D)]).then_inc(bs_in[k], 16)
            eng.wait_ge(bound_in, 16)

        @block.gpsimd
        def _(eng):
            eng.memset(xs[:, NB - 1, :], 0.0).then_inc(x_pad, 1)
            eng.memset(cf[:, :, :], 0.0).then_inc(cf_zero, 1)
            eng.iota(iti[:, :], [[1, P]], base=0, channel_multiplier=0).then_inc(io, 1)
            eng.iota(wbi[:, :], [[P, NW]], base=0, channel_multiplier=0).then_inc(io, 1)
            eng.iota(w16i[:, :], [[WD, 4]], base=0, channel_multiplier=4 * WD).then_inc(io, 1)
            eng.iota(uio[:, :], [[GRP, NRE]], base=GRP + RO, channel_multiplier=0).then_inc(io, 1)
            eng.iota(idi[:, :], [[-1, P]], base=0, channel_multiplier=1).then_inc(io, 1)

        @block.vector
        def _(eng):
            def seq(ins):
                ins.then_inc(dve_own, 1)
                take(eng, dve_own)

            eng.sem_inc(xT_psfree, 1)
            eng.sem_inc(xn_free, 1)
            eng.sem_inc(tb_out, 16)
            eng.wait_ge(io, 5)
            nc.vector.memset(g.zero[:, :], 0.0)
            nc.vector.memset(g.ones[:, :], 1.0)
            nc.vector.memset(g.one[:, :], 1.0)
            nc.vector.tensor_copy(g.iota[:, :], iti[:, :])
            nc.vector.tensor_copy(g.wbase[:, :], wbi[:, :])
            seq(nc.vector.tensor_copy(w16[:, :], w16i[:, :]))
            nc.vector.tensor_scalar(g.ident[:, :], idi[:, :], 0.0, None, ALU.is_equal).then_inc(const_ok, 1)
            eng.wait_ge(e_in, 64)
            seq(nc.vector.tensor_scalar(ka[:, :], dsti[:, :], 4, 7, ALU.logical_shift_right, ALU.logical_shift_left))
            seq(nc.vector.tensor_scalar(kb[:, :], dsti[:, :], WD - 1, None, ALU.bitwise_and))
            seq(nc.vector.scalar_tensor_tensor(out=kc[:, :], in0=eti[:, :], scalar=float(WD), in1=kb[:, :],
                                               op0=ALU.mult, op1=ALU.add))
            seq(nc.vector.tensor_tensor(g.key[:, :], kc[:, :], ka[:, :], ALU.add))
            for c in range(4):
                seq(nc.vector.tensor_scalar(before[:, :], dl[:, :], w16[:, c:c + 1], None, ALU.is_lt))
                seq(nc.vector.tensor_reduce(bf[:, c:c + 1], before[:, :], AX.X, ALU.add))
            nc.vector.tensor_copy(bi[:, :], bf[:, :]).then_inc(bi_ok, 1)
            seq(nc.vector.tensor_scalar(ush[:, :], dl[0:1, GRP - 1:NRE * GRP:GRP], 4, None, ALU.logical_shift_right))
            seq(nc.vector.tensor_tensor(g.reuse[:, :], ush[:, :], uio[:, :], ALU.add))
            eng.wait_ge(x_in, 32)
            with eng.Fori(0, NG) as c:
                xg = xs[:, ds(c * G, G), :]
                spread = lambda k: st[:, k, :].unsqueeze(2).to_broadcast([P, G, D])
                seq(nc.vector.tensor_reduce(st[:, 0, :], xg, AX.X, ALU.add))
                seq(nc.vector.tensor_scalar(st[:, 1, :], st[:, 0, :], 1.0 / D, None, ALU.mult))
                seq(nc.vector.tensor_tensor(xg, xg, spread(1), ALU.subtract))
                seq(nc.vector.tensor_tensor(sq[:, :, :], xg, xg, ALU.mult))
                seq(nc.vector.tensor_reduce(st[:, 0, :], sq[:, :, :], AX.X, ALU.add))
                nc.vector.tensor_scalar(st[:, 2, :], st[:, 0, :], 1.0 / D, EPS, ALU.mult, ALU.add).then_inc(var_ok, 1)
                take(eng, std_ok)
                seq(nc.vector.reciprocal(st[:, 1, :], st[:, 3, :]))
                take(eng, xn_free)
                seq(nc.vector.tensor_tensor(xn[:, :, :], xg, spread(1), ALU.mult))
                eng.sem_inc(xn_ok, 1)
                take(eng, tb_out, 16)
                seq(nc.vector.tensor_copy(tb[:, :, 0:D], xn[:, :, :]))
                seq(nc.vector.tensor_tensor(sq[:, :, :], xn[:, :, :], tb[:, :, 0:D], ALU.subtract))
                seq(nc.vector.tensor_copy(tb[:, :, D:2 * D], sq[:, :, :]))
                seq(nc.vector.tensor_tensor(tb[:, :, 2 * D:3 * D], sq[:, :, :], tb[:, :, D:2 * D], ALU.subtract))
                eng.sem_inc(tb_ok, 1)
            eng.wait_ge(tb_out, 16)

        @block.tensor
        def _(eng):
            eng.wait_ge(const_ok, 1)
            with eng.Fori(0, NG) as c:
                take(eng, xn_ok)
                take(eng, xT_psfree)
                for j in range(G):
                    for h in range(H2):
                        mm = nc.tensor.transpose(pT[:, j, h * P:(h + 1) * P],
                                                 xn[:, j, h * P:(h + 1) * P], g.ident[:, :])
                mm.then_inc(xT_ps, 1)
            eng.wait_ge(cf_in, 128)
            for l in range(2):
                with eng.Fori(0, NS // 2) as c:
                    for k in range(2):
                        take(eng, bs_in[k], 64)
                        take(eng, w_psfree)
                        for n in range(0, IC * D, 512):
                            mm = nc.tensor.matmul(pw[:, n:n + 512], cf[:, l, :], bs[:, k, n:n + 512],
                                                  start=True, stop=True)
                        mm.then_inc(w_ps, 1)

        @block.scalar
        def _(eng):
            eng.sem_inc(w_psfree, 1)
            eng.sem_inc(bs_free, 2)
            with eng.Fori(0, NG) as c:
                take(eng, var_ok)
                nc.scalar.activation(st[:, 3, :], st[:, 2, :], ACT.Sqrt).then_inc(std_ok, 1)
                take(eng, xT_ps)
                eng.sem_inc(xn_free, 1)
                for j in range(G):
                    ins = nc.scalar.copy(g.xT[:, :, ds((c * G + j) * P, P)],
                                         pT[:, j, :].rearrange("p (h n) -> p h n", h=H2))
                ins.then_inc(xT_psfree, 1)
                take(eng, tb_ok)
                eng.dma_start(g.table[0][ds(c * (G * P), G * P), :].rearrange("(j p) d -> p j d", p=P),
                              tb[:, :, :]).then_inc(tb_out, 16)
            for l in range(2):
                with eng.Fori(0, NS // 2) as c:
                    for k in range(2):
                        take(eng, w_ps)
                        eng.sem_inc(bs_free, 1)
                        nc.scalar.copy(wst[:, :], pw[:, :]).then_inc(w_sb, 1)
                        take(eng, w_sb)
                        eng.sem_inc(w_psfree, 1)
                        for q in range(4):
                            eng.dma_start(g.wrel[l * R:(l + 1) * R, ds(q * (D * D // 4) + (c * 2 + k) * (IC * D), IC * D)],
                                          wst[q * R:(q + 1) * R, :]).then_inc(w_out, 16)
                        take(eng, w_out, 64)


def attention(nc, g, a):
    NQ = NP // CH
    with ExitStack() as ctx:
        s = Scope(nc, ctx, "att")
        wkv = s.sb("wkv", [P, H2, 2 * D])
        wq = s.sb("wq", [P, H2, D])
        wo = s.sb("wo", [P, H2, D])
        bkv = s.sb("bkv", [P, 2 * D])
        bo = s.sb("bo", [P, D])
        bq = s.sb("bq", [P, H2])
        kt = s.sb("kt", [P, 2, D])
        ke = s.sb("ke", [P, 2, D])
        kr = s.sb("kr", [P, 2, D])
        kf = s.sb("kf", [P, 2, D])
        vb = s.sb("vb", [P, 2, H2, P + 2])
        mask = s.sb("mask", [P, P])
        kvd = s.sb("kvd", [P, H2, P])
        ksum = s.sb("ksum", [P, H2])
        ksd = s.sb("ksd", [P, H2, P])
        qe = s.sb("qe", [P, 2, CH])
        qr = s.sb("qr", [P, CH])
        qf = s.sb("qf", [P, 2, CH])
        den = s.sb("den", [P, CH])
        oT = s.sb("oT", [P, H2, NP])
        cut = s.sb("cut", [P, 2, H2, P])
        xb = s.sb("xb", [P, 2, D])
        ob = s.sb("ob", [P, 2, D])

        cut_ok, cut_free, cut2_ok, cut2_free = (s.sem(n) for n in ("cut_ok", "cut_free", "cut2_ok", "cut2_free"))
        load, mask_ok, dve_own = s.sem("load"), s.sem("mask_ok"), s.sem("dve_own")
        p_ok, p_free, kt_ok, er_ok, kf_ok, kf_free = (s.sem(n) for n in ("p_ok", "p_free", "kt_ok", "er_ok", "kf_ok", "kf_free"))
        kv_done, kvd_ok = s.sem("kv_done"), s.sem("kvd_ok")
        q_ok, q_free, qe_ok, qf_ok, nd_ok, nd_free = (s.sem(n) for n in ("q_ok", "q_free", "qe_ok", "qf_ok", "nd_ok", "nd_free"))
        oT_ok, o_ok, o_free, ob_ok, xb_free = (s.sem(n) for n in ("oT_ok", "o_ok", "o_free", "ob_ok", "xb_free"))
        xb_in = [s.sem(f"xb_in{k}") for k in range(2)]
        ob_out = [s.sem(f"ob_out{k}") for k in range(2)]
        row = lambda name: a[name].rearrange("(o d) -> o d", o=1).to_broadcast([P, D])
        mat = lambda name: a[name].rearrange("(h p) d -> p h d", p=P)

        with ExitStack() as c1:
            s1 = Scope(nc, c1, "att1")
            pk = s1.ps("pk", [P, 2, 512])
            pkv = s1.ps("pkv", [P, H2, 512])
            block = c1.enter_context(nc.Block())

            @block.sync
            def _(eng):
                eng.dma_start(wkv[:, :, 0:D], mat("L0_mix_wk")).then_inc(load, 16)
                eng.dma_start(wkv[:, :, D:2 * D], mat("L0_mix_wv")).then_inc(load, 16)
                eng.dma_start(bkv[:, 0:D], row("L0_mix_bk")).then_inc(load, 16)
                eng.dma_start(bkv[:, D:2 * D], row("L0_mix_bv")).then_inc(load, 16)
                eng.dma_start(wq[:, :, :], mat("L0_mix_wq")).then_inc(load, 16)
                eng.dma_start(wo[:, :, :], mat("L0_mix_wo")).then_inc(load, 16)
                eng.dma_start(bo[:, :], row("L0_mix_bo")).then_inc(load, 16)
                eng.dma_start(bq[:, :], a["L0_mix_bq"]).then_inc(load, 16)
                eng.wait_ge(load, 128)

            @block.gpsimd
            def _(eng):
                def copy(b, k):
                    take(eng, cut_free)
                    nc.gpsimd.tensor_copy(cut[:, k, :, :], g.xT[:, :, ds(b * P, P)]).then_inc(cut_ok, 1)

                eng.sem_inc(cut_free, 2)
                with eng.Fori(0, NB // 2) as i:
                    copy(i * 2, 0)
                    copy(i * 2 + 1, 1)
                copy(NB - 1, 0)

            @block.tensor
            def _(eng):
                def project(b, k):
                    take(eng, p_free)
                    take(eng, cut_ok)
                    for h in range(H2):
                        mm = nc.tensor.matmul(pk[:, k, :], cut[:, k, h, :], wkv[:, h, :],
                                              start=(h == 0), stop=(h == H2 - 1))
                    mm.then_inc(p_ok, 1)

                def outer(k, first=False, last=False):
                    rows = LAST if last else P
                    take(eng, kf_ok)
                    for h in range(H2):
                        mm = nc.tensor.matmul(pkv[:, h, 0:P + 2], kf[0:rows, k, h * P:(h + 1) * P], vb[0:rows, k, h, :],
                                              start=first, stop=last, skip_group_check=True)
                    mm.then_inc(kv_done if last else kf_free, 1)

                eng.wait_ge(load, 128)
                project(0, 0)
                project(1, 1)
                outer(0, first=True)
                with eng.Fori(0, (NB - 3) // 2) as i:
                    for u in range(2):
                        project(i * 2 + 2 + u, u)
                        outer((1 + u) % 2)
                project(NB - 1, 0)
                outer(1)
                outer(0, last=True)

            @block.vector
            def _(eng):
                def seq(ins):
                    ins.then_inc(dve_own, 1)
                    take(eng, dve_own)

                def block_kv(k):
                    take(eng, p_ok)
                    eng.sem_inc(cut_free, 1)
                    take(eng, kf_free)
                    seq(nc.vector.tensor_tensor(kt[:, k, :], pk[:, k, 0:D], bkv[:, 0:D], ALU.add))
                    eng.sem_inc(kt_ok, 1)
                    seq(nc.vector.tensor_tensor(vb[:, k, :, 0:P], pk[:, k, D:2 * D].rearrange("p (h n) -> p h n", h=H2),
                                                bkv[:, D:2 * D].rearrange("p (h n) -> p h n", h=H2), ALU.add))
                    eng.sem_inc(p_free, 1)
                    take(eng, er_ok)
                    nc.vector.scalar_tensor_tensor(out=kf[:, k, :], in0=ke[:, k, :], scalar=1.0, in1=kr[:, k, :],
                                                   op0=ALU.min, op1=ALU.add).then_inc(kf_ok, 1)

                eng.sem_inc(p_free, 2)
                eng.sem_inc(kf_free, 2)
                seq(nc.vector.memset(vb[:, :, :, P:P + 2], 1.0))
                seq(nc.vector.memset(mask[:, :], 0.0))
                for h in range(P // HD):
                    seq(nc.vector.memset(mask[h * HD:(h + 1) * HD, h * HD:(h + 1) * HD], 1.0))
                eng.wait_ge(load, 128)
                with eng.Fori(0, NB // 2):
                    block_kv(0)
                    block_kv(1)
                block_kv(0)
                eng.wait_ge(kv_done, 1)
                for h in range(H2):
                    seq(nc.vector.tensor_tensor(kvd[:, h, :], pkv[:, h, 0:P], mask[:, :], ALU.mult))
                    seq(nc.vector.tensor_copy(ksum[:, h:h + 1], pkv[:, h, P:P + 1]))
                    seq(nc.vector.tensor_scalar(ksd[:, h, :], mask[:, :], ksum[:, h:h + 1], None, ALU.mult))

            @block.scalar
            def _(eng):
                def block_k(k):
                    take(eng, kt_ok)
                    nc.scalar.activation(ke[:, k, :], kt[:, k, :], ACT.Exp)
                    nc.scalar.activation(kr[:, k, :], kt[:, k, :], ACT.Relu).then_inc(er_ok, 1)

                with eng.Fori(0, NB // 2):
                    block_k(0)
                    block_k(1)
                block_k(0)

        with ExitStack() as c2:
            s2 = Scope(nc, c2, "att2")
            pq = s2.ps("pq", [P, 2, 512])
            pn = s2.ps("pn", [P, 512])
            pd = s2.ps("pd", [P, 512])
            po = s2.ps("po", [P, 2, 512])
            block = c2.enter_context(nc.Block())

            @block.gpsimd
            def _(eng):
                def copy(b, k):
                    take(eng, cut2_free)
                    nc.gpsimd.tensor_copy(cut[:, k, :, :], oT[:, :, ds(b * P, P)]).then_inc(cut2_ok, 1)

                eng.wait_ge(oT_ok, 2 * NQ)
                eng.sem_inc(cut2_free, 2)
                with eng.Fori(0, NB // 2) as i:
                    copy(i * 2, 0)
                    copy(i * 2 + 1, 1)
                copy(NB - 1, 0)

            @block.tensor
            def _(eng):
                def query(c, m):
                    take(eng, q_free)
                    for h in range(H2):
                        mm = nc.tensor.matmul(pq[:, m, 0:CH], wq[:, h, m * P:(m + 1) * P], g.xT[:, h, ds(c * CH, CH)],
                                              start=(h == 0), stop=(h == H2 - 1))
                    mm.then_inc(q_ok, 1)

                def mix(m):
                    take(eng, qf_ok)
                    take(eng, nd_free)
                    nc.tensor.matmul(pn[:, 0:CH], kvd[:, m, :], qf[:, m, :], start=True, stop=True)
                    nc.tensor.matmul(pd[:, 0:CH], ksd[:, m, :], qf[:, m, :], start=True, stop=True).then_inc(nd_ok, 1)

                query(0, 0)
                with eng.Fori(0, NQ - 1) as c:
                    query(c, 1)
                    mix(0)
                    query(c + 1, 0)
                    mix(1)
                query(NQ - 1, 1)
                mix(0)
                mix(1)
                def project(b, k):
                    take(eng, o_free)
                    take(eng, cut2_ok)
                    for h in range(H2):
                        mm = nc.tensor.matmul(po[:, k, 0:D], cut[:, k, h, :], wo[:, h, :],
                                              start=(h == 0), stop=(h == H2 - 1))
                    mm.then_inc(o_ok, 1)

                with eng.Fori(0, NB // 2) as i:
                    project(i * 2, 0)
                    project(i * 2 + 1, 1)
                project(NB - 1, 0)

            @block.scalar
            def _(eng):
                with eng.Fori(0, NQ):
                    for m in range(2):
                        take(eng, q_ok)
                        nc.scalar.activation(qe[:, m, :], pq[:, m, 0:CH], ACT.Exp, bias=bq[:, m:m + 1]).then_inc(qe_ok, 1)

                def load_x(b, k, rows=P):
                    take(eng, xb_free)
                    eng.dma_start(xb[0:rows, k, :], a["x"][ds(b * P, rows), :]).then_inc(xb_in[k], 16)

                eng.sem_inc(xb_free, 2)
                load_x(0, 0)
                load_x(1, 1)

                def store(b, k):
                    take(eng, ob_ok)
                    eng.dma_start(g.base[ds(b * P, P), :], ob[:, k, :]).then_inc(ob_out[k], 16)

                with eng.Fori(0, NB // 2 - 1) as i:
                    for k in range(2):
                        store(i * 2 + k, k)
                        load_x(i * 2 + 2 + k, k)
                store(NB - 3, 0)
                load_x(NB - 1, 0, LAST)
                store(NB - 2, 1)
                store(NB - 1, 0)
                eng.wait_ge(ob_out[0], 16)
                eng.wait_ge(ob_out[1], 16)

            @block.vector
            def _(eng):
                def seq(ins):
                    ins.then_inc(dve_own, 1)
                    take(eng, dve_own)

                eng.sem_inc(q_free, 2)
                eng.sem_inc(nd_free, 1)
                eng.sem_inc(o_free, 2)
                for k in range(2):
                    eng.sem_inc(ob_out[k], 16)

                def feature(m):
                    take(eng, qe_ok)
                    seq(nc.vector.tensor_scalar(qr[:, :], pq[:, m, 0:CH], bq[:, m:m + 1], 0.0, ALU.add, ALU.max))
                    seq(nc.vector.scalar_tensor_tensor(out=qf[:, m, :], in0=qe[:, m, :], scalar=1.0, in1=qr[:, :],
                                                       op0=ALU.min, op1=ALU.add))
                    eng.sem_inc(q_free, 1)
                    eng.sem_inc(qf_ok, 1)

                def normalize(c, m):
                    take(eng, nd_ok)
                    seq(nc.vector.tensor_scalar(den[:, :], pd[:, 0:CH], 1e-6, None, ALU.add))
                    seq(nc.vector.reciprocal(den[:, :], den[:, :]))
                    seq(nc.vector.tensor_tensor(oT[:, m, ds(c * CH, CH)], pn[:, 0:CH], den[:, :], ALU.mult))
                    eng.sem_inc(nd_free, 1)
                    eng.sem_inc(oT_ok, 1)

                feature(0)
                with eng.Fori(0, NQ - 1) as c:
                    feature(1)
                    normalize(c, 0)
                    feature(0)
                    normalize(c, 1)
                feature(1)
                normalize(NQ - 1, 0)
                normalize(NQ - 1, 1)

                def finish(k):
                    take(eng, xb_in[k], 16)
                    take(eng, ob_out[k], 16)
                    seq(nc.vector.tensor_tensor(ob[:, k, :], xb[:, k, :], bo[:, :], ALU.add))
                    eng.sem_inc(xb_free, 1)
                    take(eng, o_ok)
                    eng.sem_inc(cut2_free, 1)
                    seq(nc.vector.tensor_tensor(ob[:, k, :], ob[:, k, :], po[:, k, 0:D], ALU.add))
                    eng.sem_inc(o_free, 1)
                    eng.sem_inc(ob_ok, 1)

                with eng.Fori(0, NB // 2):
                    finish(0)
                    finish(1)
                finish(0)


def gnn_layer(nc, g, a, l):
    first = l == 0
    with ExitStack() as ctx:
        s = Scope(nc, ctx, f"gnn{l}")
        ring = s.sb("ring", [P, RING, 3 * D], BF16)
        slot = s.sb("slot", [P, RING], I32)
        oh = s.sb("oh", [P, RO, P], BF16)
        wr = s.sb("wr", [P, H2, R, D])
        wself = s.sb("wself", [P, H2, D])
        parts = H2 + first
        bt = [s.sb(f"bt{k}", [P, parts, R, P]) for k in range(2)]
        xself = s.sb("xself", [P, H2, P])
        xn = s.sb("xn", [P, D])
        res = s.sb("res", [P, D])
        tb = s.sb("tb", [P, 3 * D], BF16)
        dm = s.sb("dm", [P, 1])
        bb = s.sb("bb", [P, D])
        pwin = s.ps("pwin", [P, 2, 512])
        po = s.ps("po", [P, 512])
        pdeg = s.ps("pdeg", [P, 512])
        pT = s.ps("pT", [P, 512])

        load, dve_own, slot_ok, tiles_in, pairs = (s.sem(n) for n in ("load", "dve_own", "slot_ok", "tiles_in", "pairs"))
        landed = [s.sem(f"landed{j}") for j in range(RING)]
        oh_ok, win_ok, po_ok, po_free, xn_ok, xT_ps = (s.sem(n) for n in ("oh_ok", "win_ok", "po_ok", "po_free", "xn_ok", "xT_ps"))
        win_free = [s.sem(f"win_free{k}") for k in range(2)]
        out_ok, out_done, base_in = s.sem("out_ok"), s.sem("out_done"), s.sem("base_in")
        gate = s.sem("gate")
        block = ctx.enter_context(nc.Block())

        def blocks(eng, step, tail):
            step(0, 0, False)
            with eng.Fori(0, NB // 2) as i:
                step(i * 2 + 1, 1, True)
                step(i * 2 + 2, 0, True)
            tail()

        def tiles_of(eng, w):
            return (eng.value_load(g.bound[0:1, ds(w, 1)], min_val=0, max_val=NT - 1),
                    eng.value_load(g.bound[0:1, ds(w + 1, 1)], min_val=0, max_val=NT - 1))

        @block.sync
        def _(eng):
            for h in range(H2):
                eng.dma_start(wr[:, h, :, :], g.wrel[l * R:(l + 1) * R, h * P * D:(h + 1) * P * D]
                              .rearrange("r (p o) -> p r o", p=P)).then_inc(load, 16)
            eng.dma_start(wself[:, :, :], a["L0_gnn_self_loops"][l].rearrange("(h p) o -> p h o", p=P)).then_inc(load, 16)
            with eng.Fori(0, NTP // RING) as i:
                for j in range(RING):
                    eng.wait_ge(landed[j], i * 16 + 16)
                    eng.sem_inc(tiles_in, 1)

        @block.gpsimd
        def _(eng):
            def group(i, q, wait):
                if wait:
                    last = eng.value_load(g.reuse[0:1, ds(i * (RING // GRP) + q - RING // GRP, 1)], min_val=1, max_val=2 * NTP)
                    eng.wait_ge(pairs, last)
                    eng.sem_inc(gate, 1)
                js = range(q * GRP, (q + 1) * GRP)
                nc.gpsimd.tensor_copy(slot[:, q * GRP:(q + 1) * GRP],
                                      g.idx[:, ds(i * RING + q * GRP, GRP)]).then_inc(slot_ok, 1)
                take(eng, slot_ok)
                for j in js:
                    eng.indirect_dma_start(ring[:, j, :], None, g.table[l][:, :],
                                           bass.IndirectOffsetOnAxis(ap=slot[:, j:j + 1], axis=0)).then_inc(landed[j], 16)

            for q in range(RING // GRP):
                group(0, q, False)
            with eng.Fori(1, NTP // RING) as i:
                for q in range(RING // GRP):
                    group(i, q, True)

        @block.vector
        def _(eng):
            def seq(ins):
                ins.then_inc(dve_own, 1)
                take(eng, dve_own)

            def onehots(b, j):
                w = b * WPB + j
                t0, t1 = tiles_of(eng, w)
                with eng.Fori(t0, t1 + 1) as t:
                    eng.wait_ge(pairs, t + (w + 1))
                    nc.vector.tensor_scalar(oh[:, ds((t + w) & (RO - 1), 1), :].rearrange("p o n -> p (o n)"), g.iota[:, :],
                                            g.wbase[:, ds(w, 1)], g.key[:, ds(t, 1)],
                                            ALU.add, ALU.is_equal).then_inc(oh_ok, 1)

            def finish(b):
                take(eng, po_ok)
                if first:
                    seq(nc.vector.tensor_scalar(dm[:, :], pdeg[:, 0:1], 1.0, None, ALU.max))
                    seq(nc.vector.reciprocal(g.dinv[:, ds(b, 1)], dm[:, :]))
                seq(nc.vector.tensor_scalar(xn[:, :], po[:, 0:D], g.dinv[:, ds(b, 1)], None, ALU.mult))
                seq(nc.vector.tensor_tensor(xn[:, :], xn[:, :], po[:, D:2 * D], ALU.add))
                eng.sem_inc(po_free, 1)
                take(eng, out_done, 16)
                if first:
                    seq(nc.vector.tensor_scalar(xn[:, :], xn[:, :], 0.0, None, ALU.max))
                    eng.sem_inc(xn_ok, 1)
                    seq(nc.vector.tensor_copy(tb[:, 0:D], xn[:, :]))
                    seq(nc.vector.tensor_tensor(res[:, :], xn[:, :], tb[:, 0:D], ALU.subtract))
                    seq(nc.vector.tensor_copy(tb[:, D:2 * D], res[:, :]))
                    seq(nc.vector.tensor_tensor(tb[:, 2 * D:3 * D], res[:, :], tb[:, D:2 * D], ALU.subtract))
                else:
                    take(eng, base_in, 16)
                    seq(nc.vector.tensor_tensor(res[:, :], xn[:, :], bb[:, :], ALU.add))
                eng.sem_inc(out_ok, 1)

            def step(b, k, prev):
                for j in range(WPB):
                    onehots(b, j)
                    if j == 3 and prev:
                        finish(b - 1)

            eng.sem_inc(pairs, RO)
            eng.sem_inc(po_free, 1)
            eng.sem_inc(out_done, 16)
            blocks(eng, step, lambda: finish(NB - 1))
            eng.wait_ge(out_done, 16)

        @block.tensor
        def _(eng):
            def window(b, k, j):
                w = b * WPB + j
                t0, t1 = tiles_of(eng, w)
                win = pwin[:, j % 2, :]
                take(eng, win_free[j % 2])
                nc.tensor.matmul(win[:, 0:2], g.zero[:, :], g.zero[:, 0:2], start=True, stop=False, skip_group_check=True)
                with eng.Fori(t0, t1 + 1) as t:
                    eng.wait_ge(tiles_in, t + 1)
                    take(eng, oh_ok)
                    sel = oh[:, ds((t + w) & (RO - 1), 1), :].rearrange("p o n -> p (o n)")
                    if first:
                        nc.tensor.matmul(win[:, H2 * P:(H2 + 1) * P], g.ones[:, :], sel,
                                         start=False, stop=False, skip_group_check=True)
                    for h in range(H2):
                        for part in range(3):
                            at = part * D + h * P
                            mm = nc.tensor.matmul(win[:, h * P:(h + 1) * P],
                                                  ring[:, ds(t & (RING - 1), 1), at:at + P].rearrange("p o n -> p (o n)"), sel,
                                                  start=False, stop=False, skip_group_check=True)
                    mm.then_inc(pairs, 1)
                nc.tensor.matmul(win[:, 0:2], g.zero[:, :], g.zero[:, 0:2], start=False, stop=True,
                                 skip_group_check=True).then_inc(win_ok, 1)

            def dense(b, k):
                take(eng, po_free)
                for h in range(H2):
                    for r in range(R):
                        nc.tensor.matmul(po[:, 0:D], bt[k][:, h, r, :], wr[:, h, r, :],
                                         start=(h == 0 and r == 0), stop=(h == H2 - 1 and r == R - 1))
                if first:
                    for r in range(R):
                        nc.tensor.matmul(pdeg[:, 0:1], bt[k][0:1, H2, r, :], g.one[0:1, 0:1], start=(r == 0), stop=(r == R - 1))
                for h in range(H2):
                    mm = nc.tensor.matmul(po[:, D:2 * D], xself[:, h, :], wself[:, h, :],
                                          start=(h == 0), stop=(h == H2 - 1))
                mm.then_inc(po_ok, 1)

            def transposes():
                take(eng, xn_ok)
                for h in range(H2):
                    mm = nc.tensor.transpose(pT[:, h * P:(h + 1) * P], xn[:, h * P:(h + 1) * P], g.ident[:, :])
                mm.then_inc(xT_ps, 1)

            def step(b, k, prev):
                for j in range(WPB):
                    window(b, k, j)
                    if j == 1 and prev:
                        dense(b - 1, 1 - k)
                    if j == 5 and prev and first:
                        transposes()

            def tail():
                for k in range(2):
                    take(eng, win_free[k])
                dense(NB - 1, (NB - 1) % 2)
                if first:
                    transposes()

            eng.wait_ge(load, 48)
            blocks(eng, step, tail)

        @block.scalar
        def _(eng):
            def window(b, k, j):
                take(eng, win_ok)
                if j == WPB - 1:
                    nc.scalar.copy(xself[:, :, :], g.xT[:, :, ds(b * P, P)])
                nc.scalar.copy(bt[k][:, :, :, j * WD:(j + 1) * WD],
                               pwin[:, j % 2, 0:parts * P].rearrange("p (h r n) -> p h r n", h=parts, r=R)
                               ).then_inc(win_free[j % 2], 1)

            def store(b):
                if first:
                    take(eng, xT_ps)
                    nc.scalar.copy(g.xT[:, :, ds(b * P, P)], pT[:, 0:D].rearrange("p (h n) -> p h n", h=H2))
                take(eng, out_ok)
                if first:
                    eng.dma_start(g.table[1][ds(b * P, P), :], tb[:, :]).then_inc(out_done, 16)
                else:
                    eng.dma_start(g.x2[ds(b * P, P), :], res[:, :]).then_inc(out_done, 16)

            def load_base(b):
                eng.dma_start(bb[:, :], g.base[ds(b * P, P), :]).then_inc(base_in, 16)

            def step(b, k, prev):
                for j in range(WPB):
                    window(b, k, j)
                    if j == 6:
                        if prev:
                            store(b - 1)
                        if not first:
                            load_base(b)

            for k in range(2):
                eng.sem_inc(win_free[k], 1)
            blocks(eng, step, lambda: store(NB - 1))


def ffn(nc, g, a, out):
    with ExitStack() as ctx:
        s = Scope(nc, ctx, "ffn")
        w1 = s.sb("w1", [P, H2, NC, P])
        w2 = s.sb("w2", [P, NC, D])
        b1 = s.sb("b1", [P, NC])
        b2 = s.sb("b2", [E, D])
        rw = s.sb("rw", [P, H2, E])
        rb = s.sb("rb", [P, E])
        sel = s.sb("sel", [E, NC, 2, HID], BF16)
        x2 = s.sb("x2", [P, 2, D])
        xc = s.sb("xc", [P, D])
        sq = s.sb("sq", [P, D])
        st = s.sb("st", [P, 4])
        xf = s.sb("xf", [P, D])
        xfT = s.sb("xfT", [P, 2, H2, P])
        lg = s.sb("lg", [P, E])
        mx = s.sb("mx", [P, 2])
        oh = s.sb("oh", [P, E])
        ohT = s.sb("ohT", [E, 2, P])
        omT = s.sb("omT", [E, 2, P], BF16)
        hT = s.sb("hT", [P, NC, P])
        ob = s.sb("ob", [P, 2, D])
        pT = s.ps("pT", [P, 512])
        pl = s.ps("pl", [P, 512])
        ph = s.ps("ph", [P, 2, 512])
        po = s.ps("po", [P, 512])

        load, sel_ok, sel_own, dve_own = (s.sem(n) for n in ("load", "sel_ok", "sel_own", "dve_own"))
        var_ok, std_ok, xf_ok, xT_ps, xfT_ok = (s.sem(n) for n in ("var_ok", "std_ok", "xf_ok", "xT_ps", "xfT_ok"))
        lg_ok, oh_ok, ohT_ps, ohT_ok = (s.sem(n) for n in ("lg_ok", "oh_ok", "ohT_ps", "ohT_ok"))
        h_ok, po_ok, po_free, ob_ok, x2_free = (s.sem(n) for n in ("h_ok", "po_ok", "po_free", "ob_ok", "x2_free"))
        h_free = [s.sem(f"h_free{k}") for k in range(2)]
        x2_in = [s.sem(f"x2_in{k}") for k in range(2)]
        ob_out = [s.sem(f"ob_out{k}") for k in range(2)]
        block = ctx.enter_context(nc.Block())

        def steps(eng, step):
            step(0, 0, None, None)
            with eng.Fori(0, NB // 2) as i:
                step(i * 2 + 1, 1, i * 2, 0)
                step(i * 2 + 2, 0, i * 2 + 1, 1)
            step(None, None, NB - 1, 0)

        @block.sync
        def _(eng):
            for h in range(H2):
                eng.dma_start(w1[:, h, :, :].rearrange("p c (q n) -> p (c q) n", q=2),
                              a["L0_ffn_W1"][:, h * P:(h + 1) * P, :].rearrange("e p n -> p e n")).then_inc(load, 16)
            eng.dma_start(w2[:, :, :], a["L0_ffn_W2"].rearrange("(c q) n d -> (q n) c d", q=2)).then_inc(load, 16)
            eng.dma_start(b1[:, :], a["L0_ffn_b1"]).then_inc(load, 16)
            eng.dma_start(b2[:, :], a["L0_ffn_b2"]).then_inc(load, 16)
            eng.dma_start(rw[:, :, :], a["L0_ffn_router_w"].rearrange("(h p) e -> p h e", p=P)).then_inc(load, 16)
            eng.dma_start(rb[:, :], a["L0_ffn_router_b"].rearrange("(o d) -> o d", o=1).to_broadcast([P, E])).then_inc(load, 16)

            def step(f, kf, b, kb):
                if f is not None:
                    take(eng, x2_free)
                    eng.dma_start(x2[:, kf, :], g.x2[ds(f * P, P), :]).then_inc(x2_in[kf], 16)
                if b is not None:
                    take(eng, ob_ok)
                    rows = LAST if isinstance(b, int) else P
                    eng.dma_start(out[ds(b * P, rows), :], ob[0:rows, kb, :]).then_inc(ob_out[kb], 16)

            eng.sem_inc(x2_free, 2)
            steps(eng, step)
            for k in range(2):
                eng.wait_ge(ob_out[k], 16)

        @block.gpsimd
        def _(eng):
            eng.memset(sel[:, :, :, :], 0.0).then_inc(sel_own, 1)
            eng.wait_ge(sel_own, 1)
            v = sel[:, :, :, :].rearrange("e c q n -> e (c q) n")
            eng.affine_select(out=v, in_=v, compare_op=ALU.not_equal, fill=BIG, base=0,
                              pattern=[[-1, E], [0, HID]], channel_multiplier=1).then_inc(sel_ok, 1)

        @block.vector
        def _(eng):
            def seq(ins):
                ins.then_inc(dve_own, 1)
                take(eng, dve_own)

            def step(f, kf, b, kb):
                if f is not None:
                    take(eng, x2_in[kf], 16)
                    x = x2[:, kf, :]
                    seq(nc.vector.tensor_reduce(st[:, 0:1], x, AX.X, ALU.add))
                    seq(nc.vector.tensor_scalar(st[:, 1:2], st[:, 0:1], 1.0 / D, None, ALU.mult))
                    seq(nc.vector.tensor_scalar(xc[:, :], x, st[:, 1:2], None, ALU.subtract))
                    seq(nc.vector.tensor_tensor(sq[:, :], xc[:, :], xc[:, :], ALU.mult))
                    seq(nc.vector.tensor_reduce(st[:, 0:1], sq[:, :], AX.X, ALU.add))
                    nc.vector.tensor_scalar(st[:, 2:3], st[:, 0:1], 1.0 / D, EPS, ALU.mult, ALU.add).then_inc(var_ok, 1)
                    take(eng, std_ok)
                    seq(nc.vector.reciprocal(st[:, 1:2], st[:, 3:4]))
                    seq(nc.vector.tensor_scalar(xf[:, :], xc[:, :], st[:, 1:2], None, ALU.mult))
                    eng.sem_inc(xf_ok, 1)
                    take(eng, lg_ok)
                    seq(nc.vector.tensor_tensor(lg[:, :], pl[:, 0:E], rb[:, :], ALU.add))
                    seq(nc.vector.tensor_reduce(mx[:, 0:1], lg[:, :], AX.X, ALU.max))
                    seq(nc.vector.tensor_scalar(lg[:, :], lg[:, :], mx[:, 0:1], None, ALU.is_equal))
                    seq(nc.vector.scalar_tensor_tensor(out=lg[:, :], in0=lg[:, :], scalar=-2.0 * E, in1=g.iota[:, 0:E],
                                                       op0=ALU.mult, op1=ALU.add))
                    seq(nc.vector.tensor_reduce(mx[:, 1:2], lg[:, :], AX.X, ALU.min))
                    seq(nc.vector.tensor_scalar(oh[:, :], lg[:, :], mx[:, 1:2], None, ALU.is_equal))
                    eng.sem_inc(oh_ok, 1)
                if b is not None:
                    take(eng, po_ok)
                    take(eng, ob_out[kb], 16)
                    seq(nc.vector.scalar_tensor_tensor(out=ob[:, kb, :], in0=po[:, 0:D], scalar=0.0, in1=x2[:, kb, :],
                                                       op0=ALU.max, op1=ALU.add))
                    eng.sem_inc(po_free, 1)
                    eng.sem_inc(x2_free, 1)
                    eng.sem_inc(ob_ok, 1)
                if f is not None:
                    take(eng, ohT_ps)
                    seq(nc.vector.tensor_copy(ohT[:, kf, :], pT[0:E, D:D + P]))
                    seq(nc.vector.tensor_scalar(omT[:, kf, :], pT[0:E, D:D + P], 1.0, None, ALU.subtract))
                    eng.sem_inc(ohT_ok, 1)

            eng.sem_inc(po_free, 1)
            for k in range(2):
                eng.sem_inc(ob_out[k], 16)
            eng.wait_ge(load, 112)
            steps(eng, step)

        @block.tensor
        def _(eng):
            def hidden(k, n):
                take(eng, h_free[n % 2])
                for c in range(4 * n, 4 * n + 4):
                    o = ph[:, n % 2, (c % 4) * P:(c % 4 + 1) * P]
                    for h in range(H2):
                        nc.tensor.matmul(o, w1[:, h, c, :], xfT[:, k, h, :], start=(h == 0), stop=False)
                    mm = nc.tensor.matmul(o, sel[:, c, :, :].rearrange("e q n -> e (q n)"), omT[:, k, :], start=False, stop=True)
                mm.then_inc(h_ok, 1)

            def step(f, kf, b, kb):
                if b is not None:
                    take(eng, ohT_ok)
                    hidden(kb, 0)
                    hidden(kb, 1)
                if f is not None:
                    take(eng, xf_ok)
                    for h in range(H2):
                        mm = nc.tensor.transpose(pT[:, h * P:(h + 1) * P], xf[:, h * P:(h + 1) * P], g.ident[:, :])
                    mm.then_inc(xT_ps, 1)
                if b is not None:
                    hidden(kb, 2)
                if f is not None:
                    take(eng, xfT_ok)
                    for h in range(H2):
                        mm = nc.tensor.matmul(pl[:, 0:E], xfT[:, kf, h, :], rw[:, h, :], start=(h == 0), stop=(h == H2 - 1))
                    mm.then_inc(lg_ok, 1)
                if b is not None:
                    hidden(kb, 3)
                    take(eng, po_free)
                    nc.tensor.matmul(po[:, 0:D], ohT[:, kb, :], b2[:, :], start=True, stop=False)
                    for k in range(2):
                        eng.wait_ge(h_free[k], 1)
                    for c in range(NC):
                        mm = nc.tensor.matmul(po[:, 0:D], hT[:, c, :], w2[:, c, :], start=False, stop=(c == NC - 1))
                    mm.then_inc(po_ok, 1)
                if f is not None:
                    take(eng, oh_ok)
                    nc.tensor.transpose(pT[0:E, D:D + P], oh[:, :], g.ident[:, :]).then_inc(ohT_ps, 1)

            eng.wait_ge(load, 112)
            eng.wait_ge(sel_ok, 1)
            steps(eng, step)

        @block.scalar
        def _(eng):
            def hidden(n):
                take(eng, h_ok)
                for c in range(4 * n, 4 * n + 4):
                    ins = nc.scalar.activation(hT[:, c, :], ph[:, n % 2, (c % 4) * P:(c % 4 + 1) * P], ACT.Relu,
                                               bias=b1[:, c:c + 1])
                ins.then_inc(h_free[n % 2], 1)

            def step(f, kf, b, kb):
                if f is not None:
                    take(eng, var_ok)
                    nc.scalar.activation(st[:, 3:4], st[:, 2:3], ACT.Sqrt).then_inc(std_ok, 1)
                if b is not None:
                    hidden(0)
                    hidden(1)
                if f is not None:
                    take(eng, xT_ps)
                    nc.scalar.copy(xfT[:, kf, :, :], pT[:, 0:D].rearrange("p (h n) -> p h n", h=H2)).then_inc(xfT_ok, 1)
                if b is not None:
                    hidden(2)
                    hidden(3)

            for k in range(2):
                eng.sem_inc(h_free[k], 1)
            eng.wait_ge(load, 112)
            steps(eng, step)


def program(nc, a, out):
    with ExitStack() as ctx:
        g = Shared(nc, ctx)
        prepare(nc, g, a)
        attention(nc, g, a)
        gnn_layer(nc, g, a, 0)
        gnn_layer(nc, g, a, 1)
        ffn(nc, g, a, out)


def by_partition(edges, fill):
    padded = np.full((NTP * P,), fill, edges.dtype)
    padded[:NE] = edges
    return np.ascontiguousarray(padded.reshape(NTP, P).T)


def kernel(**inputs):
    import concourse.bacc as bacc
    from concourse.bass_utils import run_bass_kernel_spmd

    layout = dict(inputs)
    layout["src"] = by_partition(np.asarray(inputs["src"]), 0)
    layout["dst"] = by_partition(np.asarray(inputs["dst"]), PAD_DST)
    layout["edge_type_8"] = by_partition(np.asarray(inputs["edge_type_8"]), 0)
    layout["L0_gnn_coeffs"] = np.asarray(inputs["L0_gnn_coeffs"]).transpose(0, 2, 1)
    layout["L0_mix_bq"] = np.asarray(inputs["L0_mix_bq"]).reshape(H2, P).T
    layout["L0_ffn_router_w"] = np.asarray(inputs["L0_ffn_router_w"]).T
    layout["L0_ffn_b1"] = np.asarray(inputs["L0_ffn_b1"]).reshape(NC, P).T

    nc = bacc.Bacc("TRN2", target_bir_lowering=False, num_devices=1)
    arrays, a = {}, {}
    for name, value in layout.items():
        value = np.ascontiguousarray(value)
        arrays[f"in_{name}"] = value
        a[name] = nc.dram_tensor(f"in_{name}", value.shape, mybir.dt.from_np(value.dtype), kind="ExternalInput").ap()
    out = nc.dram_tensor("out", (N, D), F32, kind="ExternalOutput").ap()
    program(nc, a, out)
    result = run_bass_kernel_spmd(nc, [arrays], core_ids=[0])
    return result.results[0]["out"]
```

```python
from contextlib import ExitStack

import numpy as np

import concourse.bass as bass
from concourse import mybir

F32 = mybir.dt.float32
BF16 = mybir.dt.bfloat16
I32 = mybir.dt.int32
ALU = mybir.AluOpType
ACT = mybir.ActivationFunctionType
AX = mybir.AxisListType
ds = bass.ds

P = 128
N, D = 6250, 256
NB = -(-N // P)
NP = NB * P
LAST = N - (NB - 1) * P
H2 = D // P
NE = 100000
NT = -(-NE // P)
R = 8
NBASE = 30
RW = R + 1
TPG = 4
NG = -(-NT // TPG)
NTP = NG * TPG
RG = 8
ROW = D + 4
HD = 32
CH = 448
E, HID = 32, 64
NC = E * HID // P
BIG = 1e30
EPS = 1e-5
PAD_DST = 8 * N


def take(eng, sem, n=1):
    eng.wait_ge(sem, n)
    eng.sem_inc(sem, -n)


class Scope:

    def __init__(self, nc, ctx, tag):
        self.nc, self.ctx, self.tag = nc, ctx, tag

    def sb(self, name, shape, dt=F32):
        return self.ctx.enter_context(self.nc.sbuf_tensor(f"{self.tag}_{name}", shape, dt))

    def ps(self, name, shape, dt=F32):
        return self.ctx.enter_context(self.nc.psum_tensor(f"{self.tag}_{name}", shape, dt))

    def sem(self, name):
        return self.ctx.enter_context(self.nc.semaphore(f"{self.tag}_{name}"))


class Shared:

    def __init__(self, nc, ctx):
        s = Scope(nc, ctx, "g")
        self.xT = s.sb("xT", [P, H2, NP])
        self.dst = s.sb("dst", [P, NTP])
        self.idx = s.sb("idx", [P, NTP], I32)
        self.bound = s.sb("bound", [1, P], I32)
        self.reuse = s.sb("reuse", [1, NG - RG], I32)
        self.iota = s.sb("iota", [P, P])
        self.ident = s.sb("ident", [P, P])
        self.zero = s.sb("zero", [P, P], BF16)
        self.blockno = s.sb("blockno", [P, NB])
        self.dinv = s.sb("dinv", [P, NB])
        dram = lambda name, shape, dt: nc.dram_tensor(name, shape, dt).ap()
        self.table = [dram(f"table{l}", (NP * RW, D), F32) for l in range(2)]
        self.wrel = dram("wrel", (2 * R, D * D), F32)
        self.bounds = dram("bounds", (P,), I32)
        self.base = dram("base", (NP, D), F32)
        self.x2 = dram("x2", (NP, D), F32)


def prepare(nc, g, a):
    G = 7
    NL = NB // G
    IC = 8
    NS = D // 4 // IC
    WL = 4
    with ExitStack() as ctx:
        s = Scope(nc, ctx, "pre")
        xs = s.sb("xs", [P, NB, D])
        sq = s.sb("sq", [P, G, D])
        xn = s.sb("xn", [P, G, D])
        st = s.sb("st", [P, 4, G])
        dsti = s.sb("dsti", [P, NTP], I32)
        eti = s.sb("eti", [P, NTP], I32)
        srci = s.sb("srci", [P, NTP], I32)
        dl = s.sb("dl", [P, NTP], I32)
        before = s.sb("before", [P, NG - 1])
        b128i = s.sb("b128i", [P, 1], I32)
        b128 = s.sb("b128", [P, 1])
        bf = s.sb("bf", [P, 1])
        bi = s.sb("bi", [P, 1], I32)
        iti = s.sb("iti", [P, P], I32)
        bni = s.sb("bni", [P, NB], I32)
        uio = s.sb("uio", [1, NG - RG], I32)
        ush = s.sb("ush", [1, NG - RG], I32)
        idi = s.sb("idi", [P, P], I32)
        cf = s.sb("cf", [4 * NBASE, 2, 4 * R])
        bs = s.sb("bs", [4 * NBASE, 2, IC * D])
        wst = s.sb("wst", [4 * R, IC * D])
        pT = s.ps("pT", [P, G, H2 * P])
        pw = s.ps("pw", [4 * R, IC * D])

        x_in, x_pad, e_in, io, const_ok = (s.sem(n) for n in ("x_in", "x_pad", "e_in", "io", "const_ok"))
        dve_own, var_ok, std_ok, xn_ok, xn_free = (s.sem(n) for n in ("dve_own", "var_ok", "std_ok", "xn_ok", "xn_free"))
        xT_ps, xT_psfree = s.sem("xT_ps"), s.sem("xT_psfree")
        bi_ok, bi_out, bound_in = (s.sem(n) for n in ("bi_ok", "bi_out", "bound_in"))
        cf_zero, cf_in, bs_free, w_ps, w_psfree = (s.sem(n) for n in ("cf_zero", "cf_in", "bs_free", "w_ps", "w_psfree"))
        w_sb, w_out = s.sem("w_sb"), s.sem("w_out")
        bs_in = [s.sem(f"bs_in{k}") for k in range(2)]
        bases = [a["L0_gnn_bases"][l].rearrange("b (q i) o -> q b (i o)", q=4) for l in range(2)]

        block = ctx.enter_context(nc.Block())

        def steps(eng, weights, norm):
            for l in range(2):
                with eng.Fori(0, NS // WL) as c:
                    for k in range(WL):
                        weights(l, c * WL + k, k % 2)
                    norm(c + l * (NS // WL))
            with eng.Fori(2 * NS // WL, NL) as c:
                norm(c)

        @block.sync
        def _(eng):
            eng.dma_start(xs[:, 0:G, :],
                          a["x"][0:G * P, :].rearrange("(b p) d -> p b d", p=P)).then_inc(x_in, 16)
            eng.dma_start(xs[:, G:NB - 1, :],
                          a["x"][G * P:(NB - 1) * P, :].rearrange("(b p) d -> p b d", p=P)).then_inc(x_in, 16)
            eng.wait_ge(x_pad, 1)
            eng.dma_start(xs[0:LAST, NB - 1, :], a["x"][(NB - 1) * P:N, :]).then_inc(x_in, 16)
            eng.wait_ge(cf_zero, 1)
            for l in range(2):
                for q in range(4):
                    eng.dma_start(cf[q * NBASE:(q + 1) * NBASE, l, q * R:(q + 1) * R],
                                  a["L0_gnn_coeffs"][l]).then_inc(cf_in, 16)

            def load(l, c, k):
                take(eng, bs_free)
                for q in range(4):
                    eng.dma_start(bs[q * NBASE:(q + 1) * NBASE, k, :],
                                  bases[l][q, :, ds(c * (IC * D), IC * D)]).then_inc(bs_in[k], 16)

            steps(eng, load, lambda c: None)

        @block.gpsimd
        def _(eng):
            eng.memset(xs[:, NB - 1, :], 0.0).then_inc(x_pad, 1)
            eng.memset(cf[:, :, :], 0.0).then_inc(cf_zero, 1)
            eng.iota(iti[:, :], [[1, P]], base=0, channel_multiplier=0).then_inc(io, 1)
            eng.iota(bni[:, :], [[P, NB]], base=0, channel_multiplier=0).then_inc(io, 1)
            eng.iota(b128i[:, :], [[1, 1]], base=0, channel_multiplier=P).then_inc(io, 1)
            eng.iota(uio[:, :], [[1, NG - RG]], base=1, channel_multiplier=0).then_inc(io, 1)
            eng.iota(idi[:, :], [[-1, P]], base=0, channel_multiplier=1).then_inc(io, 1)
            eng.dma_start(dsti[:, :], a["dst"]).then_inc(e_in, 16)
            eng.dma_start(eti[:, :], a["edge_type_8"]).then_inc(e_in, 16)
            eng.dma_start(srci[:, :], a["src"]).then_inc(e_in, 16)
            eng.dma_start(dl[:, :], a["dst"][P - 1:P, :].to_broadcast([P, NTP])).then_inc(e_in, 16)
            eng.wait_ge(bi_ok, 1)
            eng.dma_start(g.bounds.rearrange("(p c) -> p c", c=1), bi[:, :]).then_inc(bi_out, 16)
            eng.wait_ge(bi_out, 16)
            eng.dma_start(g.bound[:, :], g.bounds.rearrange("(a w) -> a w", a=1)).then_inc(bound_in, 16)
            eng.wait_ge(bound_in, 16)

        @block.vector
        def _(eng):
            def seq(ins):
                ins.then_inc(dve_own, 1)
                take(eng, dve_own)

            eng.sem_inc(xT_psfree, 1)
            eng.sem_inc(xn_free, 1)
            eng.wait_ge(io, 5)
            nc.vector.memset(g.zero[:, :], 0.0)
            nc.vector.tensor_copy(g.iota[:, :], iti[:, :])
            nc.vector.tensor_copy(g.blockno[:, :], bni[:, :])
            seq(nc.vector.tensor_copy(b128[:, :], b128i[:, :]))
            nc.vector.tensor_scalar(g.ident[:, :], idi[:, :], 0.0, None, ALU.is_equal).then_inc(const_ok, 1)

            def norm(c):
                xg = xs[:, ds(c * G, G), :]
                spread = lambda k: st[:, k, :].unsqueeze(2).to_broadcast([P, G, D])
                seq(nc.vector.tensor_reduce(st[:, 0, :], xg, AX.X, ALU.add))
                seq(nc.vector.tensor_scalar(st[:, 1, :], st[:, 0, :], 1.0 / D, None, ALU.mult))
                seq(nc.vector.tensor_tensor(xg, xg, spread(1), ALU.subtract))
                seq(nc.vector.tensor_tensor(sq[:, :, :], xg, xg, ALU.mult))
                seq(nc.vector.tensor_reduce(st[:, 0, :], sq[:, :, :], AX.X, ALU.add))
                nc.vector.tensor_scalar(st[:, 2, :], st[:, 0, :], 1.0 / D, EPS, ALU.mult, ALU.add).then_inc(var_ok, 1)
                take(eng, std_ok)
                seq(nc.vector.reciprocal(st[:, 1, :], st[:, 3, :]))
                take(eng, xn_free)
                seq(nc.vector.tensor_tensor(xn[:, :, :], xg, spread(1), ALU.mult))
                eng.sem_inc(xn_ok, 1)

            eng.wait_ge(x_in, 48)
            steps(eng, lambda l, c, k: None, norm)
            eng.wait_ge(e_in, 64)
            nc.vector.tensor_copy(g.dst[:, :], dsti[:, :])
            nc.vector.scalar_tensor_tensor(out=g.idx[:, :], in0=srci[:, :], scalar=float(RW), in1=eti[:, :],
                                           op0=ALU.mult, op1=ALU.add)
            last = dl[:, TPG - 1:(NG - 1) * TPG:TPG]
            seq(nc.vector.tensor_scalar(before[:, :], last, b128[:, 0:1], None, ALU.is_lt))
            seq(nc.vector.tensor_reduce(bf[:, :], before[:, :], AX.X, ALU.add))
            nc.vector.tensor_copy(bi[:, :], bf[:, :]).then_inc(bi_ok, 1)
            seq(nc.vector.tensor_scalar(ush[:, :], dl[0:1, TPG - 1:(NG - RG) * TPG:TPG], 7, None, ALU.logical_shift_right))
            seq(nc.vector.tensor_tensor(g.reuse[:, :], ush[:, :], uio[:, :], ALU.add))

        @block.tensor
        def _(eng):
            def weights(l, c, k):
                take(eng, bs_in[k], 64)
                take(eng, w_psfree)
                for n in range(0, IC * D, 512):
                    mm = nc.tensor.matmul(pw[:, n:n + 512], cf[:, l, :], bs[:, k, n:n + 512], start=True, stop=True)
                mm.then_inc(w_ps, 1)

            def norm(c):
                take(eng, xn_ok)
                take(eng, xT_psfree)
                for j in range(G):
                    for h in range(H2):
                        mm = nc.tensor.transpose(pT[:, j, h * P:(h + 1) * P], xn[:, j, h * P:(h + 1) * P], g.ident[:, :])
                mm.then_inc(xT_ps, 1)

            eng.wait_ge(const_ok, 1)
            eng.wait_ge(cf_in, 128)
            steps(eng, weights, norm)

        @block.scalar
        def _(eng):
            def weights(l, c, k):
                take(eng, w_ps)
                eng.sem_inc(bs_free, 1)
                take(eng, w_out, 64)
                nc.scalar.copy(wst[:, :], pw[:, :]).then_inc(w_sb, 1)
                take(eng, w_sb)
                eng.sem_inc(w_psfree, 1)
                for q in range(4):
                    eng.dma_start(g.wrel[l * R:(l + 1) * R, ds(c * (IC * D) + q * (D * D // 4), IC * D)],
                                  wst[q * R:(q + 1) * R, :]).then_inc(w_out, 16)

            def norm(c):
                take(eng, var_ok)
                nc.scalar.activation(st[:, 3, :], st[:, 2, :], ACT.Sqrt).then_inc(std_ok, 1)
                take(eng, xT_ps)
                eng.sem_inc(xn_free, 1)
                for j in range(G):
                    ins = nc.scalar.copy(g.xT[:, :, ds(c * (G * P) + j * P, P)],
                                         pT[:, j, :].rearrange("p (h n) -> p h n", h=H2))
                ins.then_inc(xT_psfree, 1)

            eng.sem_inc(w_psfree, 1)
            eng.sem_inc(bs_free, 2)
            eng.sem_inc(w_out, 64)
            steps(eng, weights, norm)
            eng.wait_ge(w_out, 64)


def attention(nc, g, a):
    NQ = NP // CH
    with ExitStack() as ctx:
        s = Scope(nc, ctx, "att")
        wkv = s.sb("wkv", [P, H2, 2 * D])
        wq = s.sb("wq", [P, H2, D])
        wo = s.sb("wo", [P, H2, D])
        bkv = s.sb("bkv", [P, 2 * D])
        bo = s.sb("bo", [P, D])
        bq = s.sb("bq", [P, H2])
        kt = s.sb("kt", [P, 2, D])
        ke = s.sb("ke", [P, 2, D])
        kr = s.sb("kr", [P, 2, D])
        kf = s.sb("kf", [P, 2, D])
        vb = s.sb("vb", [P, 2, H2, P + 2])
        mask = s.sb("mask", [P, P])
        kvd = s.sb("kvd", [P, H2, P])
        ksum = s.sb("ksum", [P, H2])
        ksd = s.sb("ksd", [P, H2, P])
        qe = s.sb("qe", [P, 2, CH])
        qr = s.sb("qr", [P, CH])
        qf = s.sb("qf", [P, 2, CH])
        den = s.sb("den", [P, CH])
        oT = s.sb("oT", [P, H2, NP])
        cut = s.sb("cut", [P, 2, H2, P])
        xb = s.sb("xb", [P, 2, D])
        ob = s.sb("ob", [P, 2, D])

        cut_ok, cut_free, cut2_ok, cut2_free = (s.sem(n) for n in ("cut_ok", "cut_free", "cut2_ok", "cut2_free"))
        load, mask_ok, dve_own = s.sem("load"), s.sem("mask_ok"), s.sem("dve_own")
        p_ok, p_free, kt_ok, er_ok, kf_ok, kf_free = (s.sem(n) for n in ("p_ok", "p_free", "kt_ok", "er_ok", "kf_ok", "kf_free"))
        kv_done, kvd_ok = s.sem("kv_done"), s.sem("kvd_ok")
        q_ok, q_free, qe_ok, qf_ok, nd_ok, nd_free = (s.sem(n) for n in ("q_ok", "q_free", "qe_ok", "qf_ok", "nd_ok", "nd_free"))
        oT_ok, o_ok, o_free, ob_ok, xb_free = (s.sem(n) for n in ("oT_ok", "o_ok", "o_free", "ob_ok", "xb_free"))
        xb_in = [s.sem(f"xb_in{k}") for k in range(2)]
        ob_out = [s.sem(f"ob_out{k}") for k in range(2)]
        row = lambda name: a[name].rearrange("(o d) -> o d", o=1).to_broadcast([P, D])
        mat = lambda name: a[name].rearrange("(h p) d -> p h d", p=P)

        with ExitStack() as c1:
            s1 = Scope(nc, c1, "att1")
            pk = s1.ps("pk", [P, 2, 512])
            pkv = s1.ps("pkv", [P, H2, 512])
            block = c1.enter_context(nc.Block())

            @block.sync
            def _(eng):
                eng.dma_start(wkv[:, :, 0:D], mat("L0_mix_wk")).then_inc(load, 16)
                eng.dma_start(wkv[:, :, D:2 * D], mat("L0_mix_wv")).then_inc(load, 16)
                eng.dma_start(bkv[:, 0:D], row("L0_mix_bk")).then_inc(load, 16)
                eng.dma_start(bkv[:, D:2 * D], row("L0_mix_bv")).then_inc(load, 16)
                eng.dma_start(wq[:, :, :], mat("L0_mix_wq")).then_inc(load, 16)
                eng.dma_start(wo[:, :, :], mat("L0_mix_wo")).then_inc(load, 16)
                eng.dma_start(bo[:, :], row("L0_mix_bo")).then_inc(load, 16)
                eng.dma_start(bq[:, :], a["L0_mix_bq"]).then_inc(load, 16)
                eng.wait_ge(load, 128)

            @block.gpsimd
            def _(eng):
                def copy(b, k):
                    take(eng, cut_free)
                    nc.gpsimd.tensor_copy(cut[:, k, :, :], g.xT[:, :, ds(b * P, P)]).then_inc(cut_ok, 1)

                eng.sem_inc(cut_free, 2)
                with eng.Fori(0, NB // 2) as i:
                    copy(i * 2, 0)
                    copy(i * 2 + 1, 1)
                copy(NB - 1, 0)

            @block.tensor
            def _(eng):
                def project(b, k):
                    take(eng, p_free)
                    take(eng, cut_ok)
                    for h in range(H2):
                        mm = nc.tensor.matmul(pk[:, k, :], cut[:, k, h, :], wkv[:, h, :],
                                              start=(h == 0), stop=(h == H2 - 1))
                    mm.then_inc(p_ok, 1)

                def outer(k, first=False, last=False):
                    rows = LAST if last else P
                    take(eng, kf_ok)
                    for h in range(H2):
                        mm = nc.tensor.matmul(pkv[:, h, 0:P + 2], kf[0:rows, k, h * P:(h + 1) * P], vb[0:rows, k, h, :],
                                              start=first, stop=last, skip_group_check=True)
                    mm.then_inc(kv_done if last else kf_free, 1)

                eng.wait_ge(load, 128)
                project(0, 0)
                project(1, 1)
                outer(0, first=True)
                with eng.Fori(0, (NB - 3) // 2) as i:
                    for u in range(2):
                        project(i * 2 + 2 + u, u)
                        outer((1 + u) % 2)
                project(NB - 1, 0)
                outer(1)
                outer(0, last=True)

            @block.vector
            def _(eng):
                def seq(ins):
                    ins.then_inc(dve_own, 1)
                    take(eng, dve_own)

                def block_kv(k):
                    take(eng, p_ok)
                    eng.sem_inc(cut_free, 1)
                    take(eng, kf_free)
                    seq(nc.vector.tensor_tensor(kt[:, k, :], pk[:, k, 0:D], bkv[:, 0:D], ALU.add))
                    eng.sem_inc(kt_ok, 1)
                    seq(nc.vector.tensor_tensor(vb[:, k, :, 0:P], pk[:, k, D:2 * D].rearrange("p (h n) -> p h n", h=H2),
                                                bkv[:, D:2 * D].rearrange("p (h n) -> p h n", h=H2), ALU.add))
                    eng.sem_inc(p_free, 1)
                    take(eng, er_ok)
                    nc.vector.scalar_tensor_tensor(out=kf[:, k, :], in0=ke[:, k, :], scalar=1.0, in1=kr[:, k, :],
                                                   op0=ALU.min, op1=ALU.add).then_inc(kf_ok, 1)

                eng.sem_inc(p_free, 2)
                eng.sem_inc(kf_free, 2)
                seq(nc.vector.memset(vb[:, :, :, P:P + 2], 1.0))
                seq(nc.vector.memset(mask[:, :], 0.0))
                for h in range(P // HD):
                    seq(nc.vector.memset(mask[h * HD:(h + 1) * HD, h * HD:(h + 1) * HD], 1.0))
                eng.wait_ge(load, 128)
                with eng.Fori(0, NB // 2):
                    block_kv(0)
                    block_kv(1)
                block_kv(0)
                eng.wait_ge(kv_done, 1)
                for h in range(H2):
                    seq(nc.vector.tensor_tensor(kvd[:, h, :], pkv[:, h, 0:P], mask[:, :], ALU.mult))
                    seq(nc.vector.tensor_copy(ksum[:, h:h + 1], pkv[:, h, P:P + 1]))
                    seq(nc.vector.tensor_scalar(ksd[:, h, :], mask[:, :], ksum[:, h:h + 1], None, ALU.mult))

            @block.scalar
            def _(eng):
                def block_k(k):
                    take(eng, kt_ok)
                    nc.scalar.activation(ke[:, k, :], kt[:, k, :], ACT.Exp)
                    nc.scalar.activation(kr[:, k, :], kt[:, k, :], ACT.Relu).then_inc(er_ok, 1)

                with eng.Fori(0, NB // 2):
                    block_k(0)
                    block_k(1)
                block_k(0)

        with ExitStack() as c2:
            s2 = Scope(nc, c2, "att2")
            pq = s2.ps("pq", [P, 2, 512])
            pn = s2.ps("pn", [P, 512])
            pd = s2.ps("pd", [P, 512])
            po = s2.ps("po", [P, 2, 512])
            block = c2.enter_context(nc.Block())

            @block.gpsimd
            def _(eng):
                def copy(b, k):
                    take(eng, cut2_free)
                    nc.gpsimd.tensor_copy(cut[:, k, :, :], oT[:, :, ds(b * P, P)]).then_inc(cut2_ok, 1)

                eng.wait_ge(oT_ok, 2 * NQ)
                eng.sem_inc(cut2_free, 2)
                with eng.Fori(0, NB // 2) as i:
                    copy(i * 2, 0)
                    copy(i * 2 + 1, 1)
                copy(NB - 1, 0)

            @block.tensor
            def _(eng):
                def query(c, m):
                    take(eng, q_free)
                    for h in range(H2):
                        mm = nc.tensor.matmul(pq[:, m, 0:CH], wq[:, h, m * P:(m + 1) * P], g.xT[:, h, ds(c * CH, CH)],
                                              start=(h == 0), stop=(h == H2 - 1))
                    mm.then_inc(q_ok, 1)

                def mix(m):
                    take(eng, qf_ok)
                    take(eng, nd_free)
                    nc.tensor.matmul(pn[:, 0:CH], kvd[:, m, :], qf[:, m, :], start=True, stop=True)
                    nc.tensor.matmul(pd[:, 0:CH], ksd[:, m, :], qf[:, m, :], start=True, stop=True).then_inc(nd_ok, 1)

                query(0, 0)
                with eng.Fori(0, NQ - 1) as c:
                    query(c, 1)
                    mix(0)
                    query(c + 1, 0)
                    mix(1)
                query(NQ - 1, 1)
                mix(0)
                mix(1)
                def project(b, k):
                    take(eng, o_free)
                    take(eng, cut2_ok)
                    for h in range(H2):
                        mm = nc.tensor.matmul(po[:, k, 0:D], cut[:, k, h, :], wo[:, h, :],
                                              start=(h == 0), stop=(h == H2 - 1))
                    mm.then_inc(o_ok, 1)

                with eng.Fori(0, NB // 2) as i:
                    project(i * 2, 0)
                    project(i * 2 + 1, 1)
                project(NB - 1, 0)

            @block.scalar
            def _(eng):
                with eng.Fori(0, NQ):
                    for m in range(2):
                        take(eng, q_ok)
                        nc.scalar.activation(qe[:, m, :], pq[:, m, 0:CH], ACT.Exp, bias=bq[:, m:m + 1]).then_inc(qe_ok, 1)

                def load_x(b, k, rows=P):
                    take(eng, xb_free)
                    eng.dma_start(xb[0:rows, k, :], a["x"][ds(b * P, rows), :]).then_inc(xb_in[k], 16)

                eng.sem_inc(xb_free, 2)
                load_x(0, 0)
                load_x(1, 1)

                def store(b, k):
                    take(eng, ob_ok)
                    eng.dma_start(g.base[ds(b * P, P), :], ob[:, k, :]).then_inc(ob_out[k], 16)

                with eng.Fori(0, NB // 2 - 1) as i:
                    for k in range(2):
                        store(i * 2 + k, k)
                        load_x(i * 2 + 2 + k, k)
                store(NB - 3, 0)
                load_x(NB - 1, 0, LAST)
                store(NB - 2, 1)
                store(NB - 1, 0)
                eng.wait_ge(ob_out[0], 16)
                eng.wait_ge(ob_out[1], 16)

            @block.vector
            def _(eng):
                def seq(ins):
                    ins.then_inc(dve_own, 1)
                    take(eng, dve_own)

                eng.sem_inc(q_free, 2)
                eng.sem_inc(nd_free, 1)
                eng.sem_inc(o_free, 2)
                for k in range(2):
                    eng.sem_inc(ob_out[k], 16)

                def feature(m):
                    take(eng, qe_ok)
                    seq(nc.vector.tensor_scalar(qr[:, :], pq[:, m, 0:CH], bq[:, m:m + 1], 0.0, ALU.add, ALU.max))
                    seq(nc.vector.scalar_tensor_tensor(out=qf[:, m, :], in0=qe[:, m, :], scalar=1.0, in1=qr[:, :],
                                                       op0=ALU.min, op1=ALU.add))
                    eng.sem_inc(q_free, 1)
                    eng.sem_inc(qf_ok, 1)

                def normalize(c, m):
                    take(eng, nd_ok)
                    seq(nc.vector.tensor_scalar(den[:, :], pd[:, 0:CH], 1e-6, None, ALU.add))
                    seq(nc.vector.reciprocal(den[:, :], den[:, :]))
                    seq(nc.vector.tensor_tensor(oT[:, m, ds(c * CH, CH)], pn[:, 0:CH], den[:, :], ALU.mult))
                    eng.sem_inc(nd_free, 1)
                    eng.sem_inc(oT_ok, 1)

                feature(0)
                with eng.Fori(0, NQ - 1) as c:
                    feature(1)
                    normalize(c, 0)
                    feature(0)
                    normalize(c, 1)
                feature(1)
                normalize(NQ - 1, 0)
                normalize(NQ - 1, 1)

                def finish(k):
                    take(eng, xb_in[k], 16)
                    take(eng, ob_out[k], 16)
                    seq(nc.vector.tensor_tensor(ob[:, k, :], xb[:, k, :], bo[:, :], ALU.add))
                    eng.sem_inc(xb_free, 1)
                    take(eng, o_ok)
                    eng.sem_inc(cut2_free, 1)
                    seq(nc.vector.tensor_tensor(ob[:, k, :], ob[:, k, :], po[:, k, 0:D], ALU.add))
                    eng.sem_inc(o_free, 1)
                    eng.sem_inc(ob_ok, 1)

                with eng.Fori(0, NB // 2):
                    finish(0)
                    finish(1)
                finish(0)


CHUNKS = [(n, min(n + 512, RW * D)) for n in range(0, RW * D, 512)]


def load_weights(eng, g, a, wr, l, sem):
    for h in range(H2):
        eng.dma_start(wr[:, h, 0:R, :], g.wrel[l * R:(l + 1) * R, h * P * D:(h + 1) * P * D]
                      .rearrange("r (p o) -> p r o", p=P)).then_inc(sem, 16)
    eng.dma_start(wr[:, :, R, :], a["L0_gnn_self_loops"][l].rearrange("(h p) o -> p h o", p=P)).then_inc(sem, 16)


def table_rows(g, l, b):
    return g.table[l][ds(b * (P * RW), P * RW), :].rearrange("(p r) d -> p (r d)", r=RW)


class Messages:

    def __init__(self, nc, s, g, l):
        self.nc, self.g, self.l = nc, g, l
        self.wr = s.sb("wr", [P, H2, RW, D])
        self.rows = s.sb("rows", [P, 2, RW * D])
        self.pm = s.ps("pm", [P, len(CHUNKS), 512])
        self.chunk_ok, self.chunk_free, self.rows_ok = s.sem("chunk_ok"), s.sem("chunk_free"), s.sem("rows_ok")
        self.stored = [s.sem(f"stored{k}") for k in range(2)]

    def multiply(self, eng, xT):
        for n, (lo, hi) in enumerate(CHUNKS):
            take(eng, self.chunk_free)
            for h in range(H2):
                mm = self.nc.tensor.matmul(self.pm[:, n, 0:hi - lo], xT[:, h, :],
                                           self.wr[:, h, :, :].rearrange("p r o -> p (r o)")[:, lo:hi],
                                           start=(h == 0), stop=(h == H2 - 1))
            mm.then_inc(self.chunk_ok, 1)

    def store(self, eng, b, k):
        take(eng, self.stored[k], 16)
        for n, (lo, hi) in enumerate(CHUNKS):
            take(eng, self.chunk_ok)
            ins = self.nc.scalar.copy(self.rows[:, k, lo:hi], self.pm[:, n, 0:hi - lo])
            ins.then_inc(self.chunk_free if hi < RW * D else self.rows_ok, 1)
        take(eng, self.rows_ok)
        eng.sem_inc(self.chunk_free, 1)
        eng.dma_start(table_rows(self.g, self.l, b), self.rows[:, k, :]).then_inc(self.stored[k], 16)

    def begin(self, eng):
        eng.sem_inc(self.chunk_free, len(CHUNKS))
        for k in range(2):
            eng.sem_inc(self.stored[k], 16)

    def end(self, eng):
        for k in range(2):
            eng.wait_ge(self.stored[k], 16)


def messages(nc, g, a):
    with ExitStack() as ctx:
        s = Scope(nc, ctx, "msg")
        m = Messages(nc, s, g, 0)
        cut = s.sb("cut", [P, 2, H2, P])
        load, cut_ok, cut_free = s.sem("load"), s.sem("cut_ok"), s.sem("cut_free")
        block = ctx.enter_context(nc.Block())

        def blocks(eng, step):
            with eng.Fori(0, NB // 2) as i:
                step(i * 2, 0)
                step(i * 2 + 1, 1)
            step(NB - 1, 0)

        @block.sync
        def _(eng):
            load_weights(eng, g, a, m.wr, 0, load)

        @block.gpsimd
        def _(eng):
            def step(b, k):
                take(eng, cut_free)
                nc.gpsimd.tensor_copy(cut[:, k, :, :], g.xT[:, :, ds(b * P, P)]).then_inc(cut_ok, 1)

            eng.sem_inc(cut_free, 2)
            blocks(eng, step)

        @block.tensor
        def _(eng):
            def step(b, k):
                take(eng, cut_ok)
                m.multiply(eng, cut[:, k, :, :])

            eng.wait_ge(load, 48)
            blocks(eng, step)

        @block.scalar
        def _(eng):
            def step(b, k):
                m.store(eng, b, k)
                eng.sem_inc(cut_free, 1)

            m.begin(eng)
            blocks(eng, step)
            m.end(eng)


def gnn_layer(nc, g, a, l):
    first = l == 0
    with ExitStack() as ctx:
        s = Scope(nc, ctx, f"gnn{l}")
        m = Messages(nc, s, g, 1) if first else None
        ring = s.sb("ring", [P, RG, TPG, ROW])
        slot = s.sb("slot", [P, RG * TPG], I32)
        col = s.sb("col", [P, 2, P])
        oh = s.sb("oh", [P, TPG, P])
        own = s.sb("own", [P, 2, D])
        xn = s.sb("xn", [P, D])
        xT = s.sb("xT", [P, H2, P])
        dm = s.sb("dm", [P, 1])
        base = s.sb("base", [P, 2, D])
        x2 = s.sb("x2", [P, 2, D])
        pagg = s.ps("pagg", [P, 2, 512])
        pT = s.ps("pT", [P, 512])

        load, dve_own, slot_ok, groups_in, pairs, gate = (s.sem(n) for n in ("load", "dve_own", "slot_ok", "groups_in", "pairs", "gate"))
        landed = [s.sem(f"landed{j}") for j in range(RG)]
        ring_ok = s.sem("ring_ok")
        oh_ok = [s.sem(f"oh_ok{k}") for k in range(2)]
        oh_free = [s.sem(f"oh_free{k}") for k in range(2)]
        agg_ok, xn_ok, xn_free, xT_ps, xT_ok = (s.sem(n) for n in ("agg_ok", "xn_ok", "xn_free", "xT_ps", "xT_ok"))
        agg_free = s.sem("agg_free")
        own_in = [s.sem(f"own_in{k}") for k in range(2)]
        base_in = [s.sem(f"base_in{k}") for k in range(2)]
        x2_ok = s.sem("x2_ok")
        x2_out = [s.sem(f"x2_out{k}") for k in range(2)]
        block = ctx.enter_context(nc.Block())

        def blocks(eng, step, tail=None):
            step(0, 0, False)
            with eng.Fori(0, NB // 2) as i:
                step(i * 2 + 1, 1, True)
                step(i * 2 + 2, 0, True)
            if tail:
                tail()

        def groups_of(eng, b):
            return (eng.value_load(g.bound[0:1, ds(b, 1)], min_val=0, max_val=NG - 1),
                    eng.value_load(g.bound[0:1, ds(b + 1, 1)], min_val=0, max_val=NG - 1))

        @block.sync
        def _(eng):
            if first:
                load_weights(eng, g, a, m.wr, 1, load)

            def count(i, j):
                eng.wait_ge(landed[j], i * (16 * TPG) + 16 * TPG)
                eng.sem_inc(groups_in, 1)

            with eng.Fori(0, NG // RG) as i:
                for j in range(RG):
                    count(i, j)
            for j in range(NG % RG):
                count(NG // RG, j)

        @block.gpsimd
        def _(eng):
            def group(i, j, wait):
                if wait:
                    last = eng.value_load(g.reuse[0:1, ds(i * RG + j - RG, 1)], min_val=1, max_val=NG + NB)
                    eng.wait_ge(pairs, last)
                    eng.sem_inc(gate, 1)
                mine = slice(j * TPG, (j + 1) * TPG)
                nc.gpsimd.tensor_copy(slot[:, mine], g.idx[:, ds(i * (RG * TPG) + j * TPG, TPG)]).then_inc(slot_ok, 1)
                take(eng, slot_ok)
                for t in range(TPG):
                    eng.indirect_dma_start(ring[:, j, t, 0:D], None, g.table[l][:, :],
                                           bass.IndirectOffsetOnAxis(ap=slot[:, j * TPG + t:j * TPG + t + 1], axis=0)
                                           ).then_inc(landed[j], 16)

            for j in range(RG):
                group(0, j, False)
            with eng.Fori(1, NG // RG) as i:
                for j in range(RG):
                    group(i, j, True)
            for j in range(NG % RG):
                group(NG // RG, j, True)

        @block.vector
        def _(eng):
            def seq(ins):
                ins.then_inc(dve_own, 1)
                take(eng, dve_own)

            def onehots(b, k):
                q0, q1 = groups_of(eng, b)
                seq(nc.vector.tensor_scalar(col[:, k, :], g.iota[:, :], g.blockno[:, ds(b, 1)], None, ALU.add))
                with eng.Fori(q0, q1 + 1) as q:
                    for u in range(2):
                        take(eng, oh_free[u])
                        nc.vector.tensor_tensor(oh[:, u * 2:u * 2 + 2, :],
                                                g.dst[:, ds(q * TPG + u * 2, 2)].unsqueeze(2).to_broadcast([P, 2, P]),
                                                col[:, k, :].unsqueeze(1).to_broadcast([P, 2, P]),
                                                ALU.is_equal).then_inc(oh_ok[u], 1)

            def finish(b, k):
                take(eng, agg_ok)
                if first:
                    seq(nc.vector.tensor_scalar(dm[:, :], pagg[:, k, D:D + 1], 1.0, None, ALU.max))
                    seq(nc.vector.reciprocal(g.dinv[:, ds(b, 1)], dm[:, :]))
                    take(eng, xn_free)
                take(eng, own_in[k], 16)
                seq(nc.vector.scalar_tensor_tensor(out=xn[:, :], in0=pagg[:, k, 0:D], scalar=g.dinv[:, ds(b, 1)],
                                                   in1=own[:, k, :], op0=ALU.mult, op1=ALU.add))
                eng.sem_inc(agg_free, 1)
                if first:
                    seq(nc.vector.tensor_scalar(xn[:, :], xn[:, :], 0.0, None, ALU.max))
                    eng.sem_inc(xn_ok, 1)
                else:
                    take(eng, base_in[k], 16)
                    take(eng, x2_out[k], 16)
                    seq(nc.vector.tensor_tensor(x2[:, k, :], xn[:, :], base[:, k, :], ALU.add))
                    eng.sem_inc(x2_ok, 1)

            def step(b, k, prev):
                onehots(b, k)
                finish(b, k)

            eng.sem_inc(xn_free, 1)
            eng.sem_inc(agg_free, 2)
            for k in range(2):
                eng.sem_inc(oh_free[k], 1)
                eng.sem_inc(x2_out[k], 16)
            for j in range(RG):
                ins = nc.vector.memset(ring[:, j, :, D:ROW], 1.0)
            ins.then_inc(ring_ok, 1)
            blocks(eng, step)
            for k in range(2):
                eng.wait_ge(x2_out[k], 16)

        @block.tensor
        def _(eng):
            def gather_sum(b, k):
                q0, q1 = groups_of(eng, b)
                take(eng, agg_free)
                nc.tensor.matmul(pagg[:, k, 0:2], g.zero[:, :], g.zero[:, 0:2], start=True, stop=False, skip_group_check=True)
                with eng.Fori(q0, q1 + 1) as q:
                    eng.wait_ge(groups_in, q + 1)
                    for u in range(2):
                        take(eng, oh_ok[u])
                        for t in range(u * 2, u * 2 + 2):
                            mm = nc.tensor.matmul(pagg[:, k, 0:D + 1], oh[:, t, :],
                                                  ring[:, ds(q & (RG - 1), 1), t, 0:D + 1].rearrange("p o n -> p (o n)"),
                                                  start=False, stop=False, skip_group_check=True)
                        mm.then_inc(oh_free[u], 1)
                    nc.tensor.matmul(pagg[:, k, 0:2], g.zero[:, :], g.zero[:, 0:2], start=False, stop=False,
                                     skip_group_check=True).then_inc(pairs, 1)
                nc.tensor.matmul(pagg[:, k, 0:2], g.zero[:, :], g.zero[:, 0:2], start=False, stop=True,
                                 skip_group_check=True).then_inc(agg_ok, 1)

            def transposes():
                take(eng, xn_ok)
                for h in range(H2):
                    mm = nc.tensor.transpose(pT[:, h * P:(h + 1) * P], xn[:, h * P:(h + 1) * P], g.ident[:, :])
                mm.then_inc(xT_ps, 1)

            def step(b, k, prev):
                gather_sum(b, k)
                if first:
                    if prev:
                        take(eng, xT_ok)
                        m.multiply(eng, xT)
                    transposes()

            def tail():
                if first:
                    take(eng, xT_ok)
                    m.multiply(eng, xT)

            eng.wait_ge(ring_ok, 1)
            if first:
                eng.wait_ge(load, 48)
            blocks(eng, step, tail)

        @block.scalar
        def _(eng):
            def load_own(b, k):
                rows = g.table[l][ds(b * (P * RW), P * RW), :].rearrange("(p r) d -> p r d", r=RW)
                eng.dma_start(own[:, k, :], rows[:, R, :]).then_inc(own_in[k], 16)
                if not first:
                    eng.dma_start(base[:, k, :], g.base[ds(b * P, P), :]).then_inc(base_in[k], 16)

            def step(b, k, prev):
                load_own(b, k)
                if first:
                    if prev:
                        m.store(eng, b - 1, 1 - k)
                    take(eng, xT_ps)
                    eng.sem_inc(xn_free, 1)
                    nc.scalar.copy(xT[:, :, :], pT[:, 0:D].rearrange("p (h n) -> p h n", h=H2)).then_inc(xT_ok, 1)
                else:
                    take(eng, x2_ok)
                    eng.dma_start(g.x2[ds(b * P, P), :], x2[:, k, :]).then_inc(x2_out[k], 16)


            if first:
                m.begin(eng)
            blocks(eng, step)
            if first:
                m.store(eng, NB - 1, (NB - 1) % 2)
                m.end(eng)


def ffn(nc, g, a, out):
    with ExitStack() as ctx:
        s = Scope(nc, ctx, "ffn")
        w1 = s.sb("w1", [P, H2, NC, P])
        w2 = s.sb("w2", [P, NC, D])
        b1 = s.sb("b1", [P, NC])
        b2 = s.sb("b2", [E, D])
        rw = s.sb("rw", [P, H2, E])
        rb = s.sb("rb", [P, E])
        sel = s.sb("sel", [E, NC, 2, HID], BF16)
        x2 = s.sb("x2", [P, 2, D])
        xc = s.sb("xc", [P, D])
        sq = s.sb("sq", [P, D])
        st = s.sb("st", [P, 4])
        xf = s.sb("xf", [P, D])
        xfT = s.sb("xfT", [P, 2, H2, P])
        lg = s.sb("lg", [P, E])
        mx = s.sb("mx", [P, 2])
        oh = s.sb("oh", [P, E])
        ohT = s.sb("ohT", [E, 2, P])
        omT = s.sb("omT", [E, 2, P], BF16)
        hT = s.sb("hT", [P, NC, P])
        ob = s.sb("ob", [P, 2, D])
        pT = s.ps("pT", [P, 512])
        pl = s.ps("pl", [P, 512])
        ph = s.ps("ph", [P, 2, 512])
        po = s.ps("po", [P, 512])

        load, sel_ok, sel_own, dve_own = (s.sem(n) for n in ("load", "sel_ok", "sel_own", "dve_own"))
        var_ok, std_ok, xf_ok, xT_ps, xfT_ok = (s.sem(n) for n in ("var_ok", "std_ok", "xf_ok", "xT_ps", "xfT_ok"))
        lg_ok, oh_ok, ohT_ps, ohT_ok = (s.sem(n) for n in ("lg_ok", "oh_ok", "ohT_ps", "ohT_ok"))
        h_ok, po_ok, po_free, ob_ok, x2_free = (s.sem(n) for n in ("h_ok", "po_ok", "po_free", "ob_ok", "x2_free"))
        h_free = [s.sem(f"h_free{k}") for k in range(2)]
        x2_in = [s.sem(f"x2_in{k}") for k in range(2)]
        ob_out = [s.sem(f"ob_out{k}") for k in range(2)]
        block = ctx.enter_context(nc.Block())

        def steps(eng, step):
            step(0, 0, None, None)
            with eng.Fori(0, NB // 2) as i:
                step(i * 2 + 1, 1, i * 2, 0)
                step(i * 2 + 2, 0, i * 2 + 1, 1)
            step(None, None, NB - 1, 0)

        @block.sync
        def _(eng):
            for h in range(H2):
                eng.dma_start(w1[:, h, :, :].rearrange("p c (q n) -> p (c q) n", q=2),
                              a["L0_ffn_W1"][:, h * P:(h + 1) * P, :].rearrange("e p n -> p e n")).then_inc(load, 16)
            eng.dma_start(w2[:, :, :], a["L0_ffn_W2"].rearrange("(c q) n d -> (q n) c d", q=2)).then_inc(load, 16)
            eng.dma_start(b1[:, :], a["L0_ffn_b1"]).then_inc(load, 16)
            eng.dma_start(b2[:, :], a["L0_ffn_b2"]).then_inc(load, 16)
            eng.dma_start(rw[:, :, :], a["L0_ffn_router_w"].rearrange("(h p) e -> p h e", p=P)).then_inc(load, 16)
            eng.dma_start(rb[:, :], a["L0_ffn_router_b"].rearrange("(o d) -> o d", o=1).to_broadcast([P, E])).then_inc(load, 16)

            def step(f, kf, b, kb):
                if f is not None:
                    take(eng, x2_free)
                    eng.dma_start(x2[:, kf, :], g.x2[ds(f * P, P), :]).then_inc(x2_in[kf], 16)
                if b is not None:
                    take(eng, ob_ok)
                    rows = LAST if isinstance(b, int) else P
                    eng.dma_start(out[ds(b * P, rows), :], ob[0:rows, kb, :]).then_inc(ob_out[kb], 16)

            eng.sem_inc(x2_free, 2)
            steps(eng, step)
            for k in range(2):
                eng.wait_ge(ob_out[k], 16)

        @block.gpsimd
        def _(eng):
            eng.memset(sel[:, :, :, :], 0.0).then_inc(sel_own, 1)
            eng.wait_ge(sel_own, 1)
            v = sel[:, :, :, :].rearrange("e c q n -> e (c q) n")
            eng.affine_select(out=v, in_=v, compare_op=ALU.not_equal, fill=BIG, base=0,
                              pattern=[[-1, E], [0, HID]], channel_multiplier=1).then_inc(sel_ok, 1)

        @block.vector
        def _(eng):
            def seq(ins):
                ins.then_inc(dve_own, 1)
                take(eng, dve_own)

            def step(f, kf, b, kb):
                if f is not None:
                    take(eng, x2_in[kf], 16)
                    x = x2[:, kf, :]
                    seq(nc.vector.tensor_reduce(st[:, 0:1], x, AX.X, ALU.add))
                    seq(nc.vector.tensor_scalar(st[:, 1:2], st[:, 0:1], 1.0 / D, None, ALU.mult))
                    seq(nc.vector.tensor_scalar(xc[:, :], x, st[:, 1:2], None, ALU.subtract))
                    seq(nc.vector.tensor_tensor(sq[:, :], xc[:, :], xc[:, :], ALU.mult))
                    seq(nc.vector.tensor_reduce(st[:, 0:1], sq[:, :], AX.X, ALU.add))
                    nc.vector.tensor_scalar(st[:, 2:3], st[:, 0:1], 1.0 / D, EPS, ALU.mult, ALU.add).then_inc(var_ok, 1)
                    take(eng, std_ok)
                    seq(nc.vector.reciprocal(st[:, 1:2], st[:, 3:4]))
                    seq(nc.vector.tensor_scalar(xf[:, :], xc[:, :], st[:, 1:2], None, ALU.mult))
                    eng.sem_inc(xf_ok, 1)
                    take(eng, lg_ok)
                    seq(nc.vector.tensor_tensor(lg[:, :], pl[:, 0:E], rb[:, :], ALU.add))
                    seq(nc.vector.tensor_reduce(mx[:, 0:1], lg[:, :], AX.X, ALU.max))
                    seq(nc.vector.tensor_scalar(lg[:, :], lg[:, :], mx[:, 0:1], None, ALU.is_equal))
                    seq(nc.vector.scalar_tensor_tensor(out=lg[:, :], in0=lg[:, :], scalar=-2.0 * E, in1=g.iota[:, 0:E],
                                                       op0=ALU.mult, op1=ALU.add))
                    seq(nc.vector.tensor_reduce(mx[:, 1:2], lg[:, :], AX.X, ALU.min))
                    seq(nc.vector.tensor_scalar(oh[:, :], lg[:, :], mx[:, 1:2], None, ALU.is_equal))
                    eng.sem_inc(oh_ok, 1)
                if b is not None:
                    take(eng, po_ok)
                    take(eng, ob_out[kb], 16)
                    seq(nc.vector.scalar_tensor_tensor(out=ob[:, kb, :], in0=po[:, 0:D], scalar=0.0, in1=x2[:, kb, :],
                                                       op0=ALU.max, op1=ALU.add))
                    eng.sem_inc(po_free, 1)
                    eng.sem_inc(x2_free, 1)
                    eng.sem_inc(ob_ok, 1)
                if f is not None:
                    take(eng, ohT_ps)
                    seq(nc.vector.tensor_copy(ohT[:, kf, :], pT[0:E, D:D + P]))
                    seq(nc.vector.tensor_scalar(omT[:, kf, :], pT[0:E, D:D + P], 1.0, None, ALU.subtract))
                    eng.sem_inc(ohT_ok, 1)

            eng.sem_inc(po_free, 1)
            for k in range(2):
                eng.sem_inc(ob_out[k], 16)
            eng.wait_ge(load, 112)
            steps(eng, step)

        @block.tensor
        def _(eng):
            def hidden(k, n):
                take(eng, h_free[n % 2])
                for c in range(4 * n, 4 * n + 4):
                    o = ph[:, n % 2, (c % 4) * P:(c % 4 + 1) * P]
                    for h in range(H2):
                        nc.tensor.matmul(o, w1[:, h, c, :], xfT[:, k, h, :], start=(h == 0), stop=False)
                    mm = nc.tensor.matmul(o, sel[:, c, :, :].rearrange("e q n -> e (q n)"), omT[:, k, :], start=False, stop=True)
                mm.then_inc(h_ok, 1)

            def step(f, kf, b, kb):
                if b is not None:
                    take(eng, ohT_ok)
                    hidden(kb, 0)
                    hidden(kb, 1)
                if f is not None:
                    take(eng, xf_ok)
                    for h in range(H2):
                        mm = nc.tensor.transpose(pT[:, h * P:(h + 1) * P], xf[:, h * P:(h + 1) * P], g.ident[:, :])
                    mm.then_inc(xT_ps, 1)
                if b is not None:
                    hidden(kb, 2)
                if f is not None:
                    take(eng, xfT_ok)
                    for h in range(H2):
                        mm = nc.tensor.matmul(pl[:, 0:E], xfT[:, kf, h, :], rw[:, h, :], start=(h == 0), stop=(h == H2 - 1))
                    mm.then_inc(lg_ok, 1)
                if b is not None:
                    hidden(kb, 3)
                    take(eng, po_free)
                    nc.tensor.matmul(po[:, 0:D], ohT[:, kb, :], b2[:, :], start=True, stop=False)
                    for k in range(2):
                        eng.wait_ge(h_free[k], 1)
                    for c in range(NC):
                        mm = nc.tensor.matmul(po[:, 0:D], hT[:, c, :], w2[:, c, :], start=False, stop=(c == NC - 1))
                    mm.then_inc(po_ok, 1)
                if f is not None:
                    take(eng, oh_ok)
                    nc.tensor.transpose(pT[0:E, D:D + P], oh[:, :], g.ident[:, :]).then_inc(ohT_ps, 1)

            eng.wait_ge(load, 112)
            eng.wait_ge(sel_ok, 1)
            steps(eng, step)

        @block.scalar
        def _(eng):
            def hidden(n):
                take(eng, h_ok)
                for c in range(4 * n, 4 * n + 4):
                    ins = nc.scalar.activation(hT[:, c, :], ph[:, n % 2, (c % 4) * P:(c % 4 + 1) * P], ACT.Relu,
                                               bias=b1[:, c:c + 1])
                ins.then_inc(h_free[n % 2], 1)

            def step(f, kf, b, kb):
                if f is not None:
                    take(eng, var_ok)
                    nc.scalar.activation(st[:, 3:4], st[:, 2:3], ACT.Sqrt).then_inc(std_ok, 1)
                if b is not None:
                    hidden(0)
                    hidden(1)
                if f is not None:
                    take(eng, xT_ps)
                    nc.scalar.copy(xfT[:, kf, :, :], pT[:, 0:D].rearrange("p (h n) -> p h n", h=H2)).then_inc(xfT_ok, 1)
                if b is not None:
                    hidden(2)
                    hidden(3)

            for k in range(2):
                eng.sem_inc(h_free[k], 1)
            eng.wait_ge(load, 112)
            steps(eng, step)


def program(nc, a, out):
    with ExitStack() as ctx:
        g = Shared(nc, ctx)
        prepare(nc, g, a)
        attention(nc, g, a)
        messages(nc, g, a)
        gnn_layer(nc, g, a, 0)
        gnn_layer(nc, g, a, 1)
        ffn(nc, g, a, out)


def by_partition(edges, fill):
    padded = np.full((NTP * P,), fill, edges.dtype)
    padded[:NE] = edges
    return np.ascontiguousarray(padded.reshape(NTP, P).T)


def kernel(**inputs):
    import concourse.bacc as bacc
    from concourse.bass_utils import run_bass_kernel_spmd

    layout = dict(inputs)
    layout["src"] = by_partition(np.asarray(inputs["src"]), 0)
    layout["dst"] = by_partition(np.asarray(inputs["dst"]), PAD_DST)
    layout["edge_type_8"] = by_partition(np.asarray(inputs["edge_type_8"]), 0)
    layout["L0_gnn_coeffs"] = np.asarray(inputs["L0_gnn_coeffs"]).transpose(0, 2, 1)
    layout["L0_mix_bq"] = np.asarray(inputs["L0_mix_bq"]).reshape(H2, P).T
    layout["L0_ffn_router_w"] = np.asarray(inputs["L0_ffn_router_w"]).T
    layout["L0_ffn_b1"] = np.asarray(inputs["L0_ffn_b1"]).reshape(NC, P).T

    nc = bacc.Bacc("TRN2", target_bir_lowering=False, num_devices=1)
    arrays, a = {}, {}
    for name, value in layout.items():
        value = np.ascontiguousarray(value)
        arrays[f"in_{name}"] = value
        a[name] = nc.dram_tensor(f"in_{name}", value.shape, mybir.dt.from_np(value.dtype), kind="ExternalInput").ap()
    out = nc.dram_tensor("out", (N, D), F32, kind="ExternalOutput").ap()
    program(nc, a, out)
    result = run_bass_kernel_spmd(nc, [arrays], core_ids=[0])
    return result.results[0]["out"]
```

```python
from contextlib import ExitStack

import numpy as np

import concourse.bass as bass
from concourse import mybir

F32 = mybir.dt.float32
F32R = mybir.dt.float32r
BF16 = mybir.dt.bfloat16
I32 = mybir.dt.int32
ALU = mybir.AluOpType
ACT = mybir.ActivationFunctionType
AX = mybir.AxisListType
ds = bass.ds

P = 128
N, D = 6250, 256
NB = -(-N // P)
NP = NB * P
LAST = N - (NB - 1) * P
H2 = D // P
NE = 100000
NT = -(-NE // P)
R = 8
NBASE = 30
RW = R + 1
TPG = 4
NG = -(-NT // TPG)
NTP = NG * TPG
RG = 8
ROW = D + 4
HD = 32
E, HID = 32, 64
MAXT = (NP + E * (P - 1)) // P
TU = 4
EPS = 1e-5
PAD_DST = 8 * N
assert MAXT % TU == 0


def take(eng, sem, n=1):
    eng.wait_ge(sem, n)
    eng.sem_inc(sem, -n)


class Scope:

    def __init__(self, nc, ctx, tag):
        self.nc, self.ctx, self.tag = nc, ctx, tag

    def sb(self, name, shape, dt=F32):
        return self.ctx.enter_context(self.nc.sbuf_tensor(f"{self.tag}_{name}", shape, dt))

    def ps(self, name, shape, dt=F32):
        return self.ctx.enter_context(self.nc.psum_tensor(f"{self.tag}_{name}", shape, dt))

    def sem(self, name):
        return self.nc.alloc_semaphore(f"{self.tag}_{name}")


def blocks_in_twos(eng, step):
    step(0, 0, False)
    with eng.Fori(0, NB // 2) as i:
        step(i * 2 + 1, 1, True)
        step(i * 2 + 2, 0, True)


class Shared:

    def __init__(self, nc, ctx):
        s = Scope(nc, ctx, "g")
        self.xT = s.sb("xT", [P, H2, NP])
        self.dst = s.sb("dst", [P, NTP + TPG])
        self.idx = s.sb("idx", [P, NTP], I32)
        self.bound = s.sb("bound", [1, P], I32)
        self.reuse = s.sb("reuse", [1, NG - RG], I32)
        self.iota = s.sb("iota", [P, P])
        self.ident = s.sb("ident", [P, P])
        self.zero = s.sb("zero", [P, P], BF16)
        self.blockno = s.sb("blockno", [P, NB + 1])
        self.dinv = s.sb("dinv", [P, NB])
        self.e_in, self.bi_out, self.bound_in, self.scattered = (s.sem(n) for n in ("e_in", "bi_out", "bound_in", "scattered"))
        self.landed = [[s.sem(f"landed{l}_{j}") for j in range(RG)] for l in range(2)]
        self.landed_back = [s.sem(f"landed_back{j}") for j in range(RG)]
        self.dve_own = s.sem("dve_own")
        self.xT_ps, self.xT_ok = s.sem("xT_ps"), s.sem("xT_ok")
        self.moved = [s.sem(f"moved{k}") for k in range(2)]
        self.agg_sems = {n: s.sem(n) for n in ("slot_ok", "groups_in", "gate", "ring_ok", "agg_ok", "agg_free",
                                               *(f"oh_ok{t}" for t in range(TPG)), *(f"oh_free{t}" for t in range(TPG)))}
        dram = lambda name, shape, dt: nc.dram_tensor(name, shape, dt).ap()
        self.table = [dram(f"table{l}", (NP * RW, D), F32) for l in range(2)]
        self.wrel = dram("wrel", (2 * R, D * D), F32)
        self.bounds = dram("bounds", (P,), I32)
        self.base = dram("base", (NP, D), F32)
        self.bucket = dram("bucket", ((MAXT + TU) * P, D), F32)
        self.routed = dram("routed", (MAXT * P, D), F32)


def prepare(nc, g, a):
    G = 7
    NL = NB // G
    IC = 8
    NS = D // 4 // IC
    HALVES = [slice(0, IC * D // 2), slice(IC * D // 2, IC * D)]
    with ExitStack() as ctx:
        s = Scope(nc, ctx, "pre")
        xs = s.sb("xs", [P, NB, D])
        sq = s.sb("sq", [P, G, D])
        xn = s.sb("xn", [P, G, D])
        st = s.sb("st", [P, 4, G])
        dsti = s.sb("dsti", [P, NTP], I32)
        eti = s.sb("eti", [P, NTP], I32)
        srci = s.sb("srci", [P, NTP], I32)
        dl = s.sb("dl", [P, NTP], I32)
        before = s.sb("before", [P, NG - 1])
        b128i = s.sb("b128i", [P, 1], I32)
        b128 = s.sb("b128", [P, 1])
        bf = s.sb("bf", [P, 1])
        bi = s.sb("bi", [P, 1], I32)
        iti = s.sb("iti", [P, P], I32)
        bni = s.sb("bni", [P, NB + 1], I32)
        uio = s.sb("uio", [1, NG - RG], I32)
        ush = s.sb("ush", [1, NG - RG], I32)
        idi = s.sb("idi", [P, P], I32)
        cf = s.sb("cf", [4 * NBASE, 2, 4 * R])
        bs = s.sb("bs", [4 * NBASE, 2, IC * D])
        wst = s.sb("wst", [4 * R, 2, IC * D])
        pT = s.ps("pT", [P, G, H2 * P])
        pw = s.ps("pw", [4 * R, IC * D])

        x_in, x_pad, io, const_ok = (s.sem(n) for n in ("x_in", "x_pad", "io", "const_ok"))
        e_in, bi_out, bound_in = g.e_in, g.bi_out, g.bound_in
        dve_own = g.dve_own
        var_ok, std_ok, xn_ok, xn_free = (s.sem(n) for n in ("var_ok", "std_ok", "xn_ok", "xn_free"))
        xT_ps, xT_psfree = s.sem("xT_ps"), s.sem("xT_psfree")
        bi_ok = s.sem("bi_ok")
        cf_zero, cf_in, bs_free, w_ps, w_psfree = (s.sem(n) for n in ("cf_zero", "cf_in", "bs_free", "w_ps", "w_psfree"))
        w_sb, w_out = s.sem("w_sb"), g.moved
        bs_in = [s.sem(f"bs_in{k}") for k in range(2)]
        bases = [a["L0_gnn_bases"][l].rearrange("b (q i) o -> q b (i o)", q=4) for l in range(2)]

        block = ctx.enter_context(nc.Block())

        def steps(eng, weights, norm):
            done = 0
            for l in range(2):
                n = min(NS // 2, NL - done)
                with eng.Fori(0, n) as c:
                    for k in range(2):
                        weights(l, c * 2 + k, k)
                    norm(c + done)
                for c in range(2 * n, NS):
                    weights(l, c, c % 2)
                done += n

        @block.sync
        def _(eng):
            eng.dma_start(xs[:, 0:G, :],
                          a["x"][0:G * P, :].rearrange("(b p) d -> p b d", p=P)).then_inc(x_in, 16)
            eng.dma_start(xs[:, G:NB - 1, :],
                          a["x"][G * P:(NB - 1) * P, :].rearrange("(b p) d -> p b d", p=P)).then_inc(x_in, 16)
            eng.wait_ge(x_pad, 1)
            eng.dma_start(xs[0:LAST, NB - 1, :], a["x"][(NB - 1) * P:N, :]).then_inc(x_in, 16)
            eng.wait_ge(cf_zero, 1)
            for l in range(2):
                for q in range(4):
                    eng.dma_start(cf[q * NBASE:(q + 1) * NBASE, l, q * R:(q + 1) * R],
                                  a["L0_gnn_coeffs"][l]).then_inc(cf_in, 16)

            def load(l, c, k):
                take(eng, bs_free)
                for q in range(4):
                    eng.dma_start(bs[q * NBASE:(q + 1) * NBASE, k, :],
                                  bases[l][q, :, ds(c * (IC * D), IC * D)]).then_inc(bs_in[k], 16)

            steps(eng, load, lambda c: None)

        @block.gpsimd
        def _(eng):
            eng.memset(xs[:, NB - 1, :], 0.0).then_inc(x_pad, 1)
            eng.memset(cf[:, :, :], 0.0).then_inc(cf_zero, 1)
            eng.iota(iti[:, :], [[1, P]], base=0, channel_multiplier=0).then_inc(io, 1)
            eng.iota(bni[:, :], [[P, NB + 1]], base=0, channel_multiplier=0).then_inc(io, 1)
            eng.iota(b128i[:, :], [[1, 1]], base=0, channel_multiplier=P).then_inc(io, 1)
            eng.iota(uio[:, :], [[1, NG - RG]], base=1, channel_multiplier=0).then_inc(io, 1)
            eng.iota(idi[:, :], [[-1, P]], base=0, channel_multiplier=1).then_inc(io, 1)
            eng.dma_start(dsti[:, :], a["dst"]).then_inc(e_in, 16)
            eng.dma_start(eti[:, :], a["edge_type_8"]).then_inc(e_in, 16)
            eng.dma_start(srci[:, :], a["src"]).then_inc(e_in, 16)
            eng.dma_start(dl[:, :], a["dst"][P - 1:P, :].to_broadcast([P, NTP])).then_inc(e_in, 16)
            eng.wait_ge(bi_ok, 1)
            eng.dma_start(g.bounds.rearrange("(p c) -> p c", c=1), bi[:, :]).then_inc(bi_out, 16)
            eng.wait_ge(bi_out, 16)
            eng.dma_start(g.bound[:, :], g.bounds.rearrange("(a w) -> a w", a=1)).then_inc(bound_in, 16)
            eng.wait_ge(bound_in, 16)

        @block.vector
        def _(eng):
            def seq(ins):
                ins.then_inc(dve_own, 1)
                take(eng, dve_own)

            eng.sem_inc(xT_psfree, 1)
            eng.sem_inc(xn_free, 1)
            eng.wait_ge(io, 5)
            nc.vector.memset(g.zero[:, :], 0.0)
            nc.vector.tensor_copy(g.iota[:, :], iti[:, :])
            nc.vector.tensor_copy(g.blockno[:, :], bni[:, :])
            seq(nc.vector.tensor_copy(b128[:, :], b128i[:, :]))
            nc.vector.tensor_scalar(g.ident[:, :], idi[:, :], 0.0, None, ALU.is_equal).then_inc(const_ok, 1)

            def norm(c):
                xg = xs[:, ds(c * G, G), :]
                spread = lambda k: st[:, k, :].unsqueeze(2).to_broadcast([P, G, D])
                seq(nc.vector.tensor_reduce(st[:, 0, :], xg, AX.X, ALU.add))
                seq(nc.vector.tensor_scalar(st[:, 1, :], st[:, 0, :], 1.0 / D, None, ALU.mult))
                seq(nc.vector.tensor_tensor(xg, xg, spread(1), ALU.subtract))
                seq(nc.vector.tensor_tensor(sq[:, :, :], xg, xg, ALU.mult))
                seq(nc.vector.tensor_reduce(st[:, 0, :], sq[:, :, :], AX.X, ALU.add))
                nc.vector.tensor_scalar(st[:, 2, :], st[:, 0, :], 1.0 / D, EPS, ALU.mult, ALU.add).then_inc(var_ok, 1)
                take(eng, std_ok)
                seq(nc.vector.reciprocal(st[:, 1, :], st[:, 3, :]))
                take(eng, xn_free)
                seq(nc.vector.tensor_tensor(xn[:, :, :], xg, spread(1), ALU.mult))
                eng.sem_inc(xn_ok, 1)

            eng.wait_ge(x_in, 48)
            steps(eng, lambda l, c, k: None, norm)
            eng.wait_ge(e_in, 64)
            nc.vector.tensor_copy(g.dst[:, 0:NTP], dsti[:, :])
            nc.vector.scalar_tensor_tensor(out=g.idx[:, :], in0=srci[:, :], scalar=float(RW), in1=eti[:, :],
                                           op0=ALU.mult, op1=ALU.add)
            last = dl[:, TPG - 1:(NG - 1) * TPG:TPG]
            seq(nc.vector.tensor_scalar(before[:, :], last, b128[:, 0:1], None, ALU.is_lt))
            seq(nc.vector.tensor_reduce(bf[:, :], before[:, :], AX.X, ALU.add))
            nc.vector.tensor_copy(bi[:, :], bf[:, :]).then_inc(bi_ok, 1)
            seq(nc.vector.tensor_scalar(ush[:, :], dl[0:1, TPG - 1:(NG - RG) * TPG:TPG], 7, None, ALU.logical_shift_right))
            seq(nc.vector.tensor_tensor(g.reuse[:, :], ush[:, :], uio[:, :], ALU.add))

        @block.tensor
        def _(eng):
            def weights(l, c, k):
                take(eng, bs_in[k], 64)
                for half in HALVES:
                    take(eng, w_psfree)
                    for n in range(half.start, half.stop, 512):
                        mm = nc.tensor.matmul(pw[:, n:n + 512], cf[:, l, :], bs[:, k, n:n + 512], start=True, stop=True)
                    mm.then_inc(w_ps, 1)

            def norm(c):
                take(eng, xn_ok)
                take(eng, xT_psfree)
                for j in range(G):
                    for h in range(H2):
                        mm = nc.tensor.transpose(pT[:, j, h * P:(h + 1) * P], xn[:, j, h * P:(h + 1) * P], g.ident[:, :])
                mm.then_inc(xT_ps, 1)

            eng.wait_ge(const_ok, 1)
            eng.wait_ge(cf_in, 128)
            steps(eng, weights, norm)

        @block.scalar
        def _(eng):
            def weights(l, c, k):
                take(eng, w_out[k], 64)
                for half in HALVES:
                    take(eng, w_ps)
                    nc.scalar.copy(wst[:, k, half], pw[:, half]).then_inc(w_sb, 1)
                    if half is HALVES[1]:
                        eng.sem_inc(bs_free, 1)
                    take(eng, w_sb)
                    eng.sem_inc(w_psfree, 1)
                for q in range(4):
                    eng.dma_start(g.wrel[l * R:(l + 1) * R, ds(c * (IC * D) + q * (D * D // 4), IC * D)],
                                  wst[q * R:(q + 1) * R, k, :]).then_inc(w_out[k], 16)

            def norm(c):
                take(eng, var_ok)
                nc.scalar.activation(st[:, 3, :], st[:, 2, :], ACT.Sqrt).then_inc(std_ok, 1)
                take(eng, xT_ps)
                eng.sem_inc(xn_free, 1)
                for j in range(G):
                    ins = nc.scalar.copy(g.xT[:, :, ds(c * (G * P) + j * P, P)],
                                         pT[:, j, :].rearrange("p (h n) -> p h n", h=H2))
                ins.then_inc(xT_psfree, 1)

            eng.sem_inc(w_psfree, 2)
            eng.sem_inc(bs_free, 2)
            for k in range(2):
                eng.sem_inc(w_out[k], 64)
            steps(eng, weights, norm)
            for k in range(2):
                take(eng, w_out[k], 64)


def attention(nc, g, a):
    with ExitStack() as ctx:
        s = Scope(nc, ctx, "att")
        wkv = s.sb("wkv", [P, H2, 2 * D])
        wq = s.sb("wq", [P, H2, D])
        wo = s.sb("wo", [P, H2, D])
        bkv = s.sb("bkv", [P, 2 * D])
        bo = s.sb("bo", [P, D])
        bq = s.sb("bq", [P, H2])
        kt = s.sb("kt", [P, 2, D])
        ke = s.sb("ke", [P, 2, D])
        kr = s.sb("kr", [P, 2, D])
        kf = s.sb("kf", [P, 2, D])
        vb = s.sb("vb", [P, 2, H2, P + 2])
        mask = s.sb("mask", [P, P])
        kvd = s.sb("kvd", [P, H2, P])
        ksum = s.sb("ksum", [P, H2])
        ksd = s.sb("ksd", [P, H2, P])
        cut = s.sb("cut", [P, 2, H2, P])
        zrow = s.sb("zrow", [P, D])

        zrow_ok, zeroed = s.sem("zrow_ok"), s.sem("zeroed")
        cut_ok, cut_free = s.sem("cut_ok"), s.sem("cut_free")
        load, dve_own = s.sem("load"), g.dve_own
        p_ok, p_free, kt_ok, er_ok, kf_ok, kf_free = (s.sem(n) for n in ("p_ok", "p_free", "kt_ok", "er_ok", "kf_ok", "kf_free"))
        kv_done = s.sem("kv_done")
        row = lambda name: a[name].rearrange("(o d) -> o d", o=1).to_broadcast([P, D])
        mat = lambda name: a[name].rearrange("(h p) d -> p h d", p=P)

        with ExitStack() as c1:
            s1 = Scope(nc, c1, "att1")
            pk = s1.ps("pk", [P, 2, 512])
            pkv = s1.ps("pkv", [P, H2, 512])
            block = c1.enter_context(nc.Block())

            @block.sync
            def _(eng):
                eng.dma_start(wkv[:, :, 0:D], mat("L0_mix_wk")).then_inc(load, 16)
                eng.dma_start(wkv[:, :, D:2 * D], mat("L0_mix_wv")).then_inc(load, 16)
                eng.dma_start(bkv[:, 0:D], row("L0_mix_bk")).then_inc(load, 16)
                eng.dma_start(bkv[:, D:2 * D], row("L0_mix_bv")).then_inc(load, 16)
                eng.dma_start(wq[:, :, :], mat("L0_mix_wq")).then_inc(load, 16)
                eng.dma_start(wo[:, :, :], mat("L0_mix_wo")).then_inc(load, 16)
                eng.dma_start(bo[:, :], row("L0_mix_bo")).then_inc(load, 16)
                eng.dma_start(bq[:, :], a["L0_mix_bq"]).then_inc(load, 16)
                eng.wait_ge(zrow_ok, 1)
                eng.dma_start(g.bucket.rearrange("(t p) d -> p t d", p=P),
                              zrow[:, :].unsqueeze(1).to_broadcast([P, MAXT + TU, D])).then_inc(zeroed, 16)
                eng.dma_start(g.routed[NB * P:MAXT * P, :].rearrange("(t p) d -> p t d", p=P),
                              zrow[:, :].unsqueeze(1).to_broadcast([P, MAXT - NB, D])).then_inc(zeroed, 16)
                eng.wait_ge(zeroed, 32)
                eng.wait_ge(load, 128)

            @block.gpsimd
            def _(eng):
                nc.gpsimd.memset(zrow[:, :], 0.0).then_inc(zrow_ok, 1)

                def copy(b, k):
                    take(eng, cut_free)
                    nc.gpsimd.tensor_copy(cut[:, k, :, :], g.xT[:, :, ds(b * P, P)]).then_inc(cut_ok, 1)

                eng.sem_inc(cut_free, 2)
                with eng.Fori(0, NB // 2) as i:
                    copy(i * 2, 0)
                    copy(i * 2 + 1, 1)
                copy(NB - 1, 0)

            @block.tensor
            def _(eng):
                def project(b, k):
                    take(eng, p_free)
                    take(eng, cut_ok)
                    for h in range(H2):
                        mm = nc.tensor.matmul(pk[:, k, :], cut[:, k, h, :], wkv[:, h, :],
                                              start=(h == 0), stop=(h == H2 - 1))
                    mm.then_inc(p_ok, 1)

                def outer(k, first=False, last=False):
                    rows = LAST if last else P
                    take(eng, kf_ok)
                    for h in range(H2):
                        mm = nc.tensor.matmul(pkv[:, h, 0:P + 2], kf[0:rows, k, h * P:(h + 1) * P], vb[0:rows, k, h, :],
                                              start=first, stop=last, skip_group_check=True)
                    mm.then_inc(kv_done if last else kf_free, 1)

                eng.wait_ge(load, 128)
                project(0, 0)
                project(1, 1)
                project(2, 0)
                outer(0, first=True)
                with eng.Fori(0, (NB - 3) // 2) as i:
                    for u in range(2):
                        project(i * 2 + 3 + u, 1 - u)
                        outer(1 - u)
                outer(1)
                outer(0, last=True)

            @block.vector
            def _(eng):
                def seq(ins):
                    ins.then_inc(dve_own, 1)
                    take(eng, dve_own)

                def front(k):
                    take(eng, p_ok)
                    eng.sem_inc(cut_free, 1)
                    take(eng, kf_free)
                    nc.vector.tensor_tensor(kt[:, k, :], pk[:, k, 0:D], bkv[:, 0:D], ALU.add).then_inc(kt_ok, 1)
                    nc.vector.tensor_tensor(vb[:, k, :, 0:P], pk[:, k, D:2 * D].rearrange("p (h n) -> p h n", h=H2),
                                            bkv[:, D:2 * D].rearrange("p (h n) -> p h n", h=H2), ALU.add).then_inc(p_free, 1)

                def back(k):
                    take(eng, er_ok)
                    nc.vector.scalar_tensor_tensor(out=kf[:, k, :], in0=ke[:, k, :], scalar=1.0, in1=kr[:, k, :],
                                                   op0=ALU.min, op1=ALU.add).then_inc(kf_ok, 1)

                eng.sem_inc(p_free, 2)
                eng.sem_inc(kf_free, 2)
                seq(nc.vector.memset(vb[:, :, :, P:P + 2], 1.0))
                seq(nc.vector.memset(mask[:, :], 0.0))
                for h in range(P // HD):
                    seq(nc.vector.memset(mask[h * HD:(h + 1) * HD, h * HD:(h + 1) * HD], 1.0))
                eng.wait_ge(load, 128)
                front(0)
                with eng.Fori(0, NB // 2):
                    for k in range(2):
                        front(1 - k)
                        back(k)
                back(0)
                eng.wait_ge(kv_done, 1)
                for h in range(H2):
                    seq(nc.vector.tensor_tensor(kvd[:, h, :], pkv[:, h, 0:P], mask[:, :], ALU.mult))
                    seq(nc.vector.tensor_copy(ksum[:, h:h + 1], pkv[:, h, P:P + 1]))
                    seq(nc.vector.tensor_scalar(ksd[:, h, :], mask[:, :], ksum[:, h:h + 1], None, ALU.mult))

            @block.scalar
            def _(eng):
                def block_k(k):
                    take(eng, kt_ok)
                    nc.scalar.activation(ke[:, k, :], kt[:, k, :], ACT.Exp)
                    nc.scalar.activation(kr[:, k, :], kt[:, k, :], ACT.Relu).then_inc(er_ok, 1)

                with eng.Fori(0, NB // 2):
                    block_k(0)
                    block_k(1)
                block_k(0)

        with ExitStack() as c2:
            queries_and_messages(nc, g, a, c2, wq, wo, bq, bo, kvd, ksd)


CHUNKS = [(n, min(n + 512, RW * D)) for n in range(0, RW * D, 512)]


def load_weights(eng, g, a, wr, l, sem):
    for h in range(H2):
        eng.dma_start(wr[:, h, 0:R, :], g.wrel[l * R:(l + 1) * R, h * P * D:(h + 1) * P * D]
                      .rearrange("r (p o) -> p r o", p=P)).then_inc(sem, 16)
    eng.dma_start(wr[:, :, R, :], a["L0_gnn_self_loops"][l].rearrange("(h p) o -> p h o", p=P)).then_inc(sem, 16)


def table_rows(g, l, b):
    return g.table[l][ds(b * (P * RW), P * RW), :].rearrange("(p r) d -> p (r d)", r=RW)


class Messages:

    def __init__(self, nc, s, g, l):
        self.nc, self.g, self.l = nc, g, l
        self.wr = s.sb("wr", [P, H2, RW, D])
        self.rows = s.sb("rows", [P, 2, RW * D])
        self.pm = s.ps("pm", [P, len(CHUNKS), 512])
        self.chunk_ok, self.chunk_free, self.rows_ok = s.sem("chunk_ok"), s.sem("chunk_free"), s.sem("rows_ok")
        self.stored = [s.sem(f"stored{k}") for k in range(2)]

    def multiply(self, eng, xT, first=0, end=len(CHUNKS)):
        for n in range(first, end):
            lo, hi = CHUNKS[n]
            take(eng, self.chunk_free)
            for h in range(H2):
                mm = self.nc.tensor.matmul(self.pm[:, n, 0:hi - lo], xT[:, h, :],
                                           self.wr[:, h, :, :].rearrange("p r o -> p (r o)")[:, lo:hi],
                                           start=(h == 0), stop=(h == H2 - 1))
            mm.then_inc(self.chunk_ok, 1)

    def multiply_split(self, eng, x, w, first=0, end=len(CHUNKS)):
        for n in range(first, end):
            lo, hi = CHUNKS[n]
            take(eng, self.chunk_free)
            for h in range(H2):
                for i, j in ((0, 0), (0, 1), (1, 0)):
                    mm = self.nc.tensor.matmul(self.pm[:, n, 0:hi - lo], x[i][:, h, :], w[j][:, h, lo:hi],
                                               start=(h == i + j == 0), stop=(h == H2 - 1 and i == 1))
            mm.then_inc(self.chunk_ok, 1)

    def store(self, eng, b, k):
        take(eng, self.stored[k], 16)
        for n, (lo, hi) in enumerate(CHUNKS):
            take(eng, self.chunk_ok)
            ins = self.nc.scalar.copy(self.rows[:, k, lo:hi], self.pm[:, n, 0:hi - lo])
            ins.then_inc(self.chunk_free if hi < RW * D else self.rows_ok, 1)
        take(eng, self.rows_ok)
        eng.sem_inc(self.chunk_free, 1)
        eng.dma_start(table_rows(self.g, self.l, b), self.rows[:, k, :]).then_inc(self.stored[k], 16)

    def begin(self, eng):
        eng.sem_inc(self.chunk_free, len(CHUNKS))
        for k in range(2):
            eng.sem_inc(self.stored[k], 16)

    def end(self, eng):
        for k in range(2):
            eng.wait_ge(self.stored[k], 16)


def blocks_ahead(eng, step):
    step(0, 0, False, False)
    with eng.Fori(0, NB // 2 - 1) as i:
        step(i * 2 + 1, 1, True, False)
        step(i * 2 + 2, 0, True, False)
    step(NB - 2, 1, True, False)
    step(NB - 1, 0, True, True)


def queries_and_messages(nc, g, a, ctx, wq, wo, bq, bo, kvd, ksd):
    s = Scope(nc, ctx, "msg")
    m = Messages(nc, s, g, 0)
    cut = s.sb("cut", [P, 2, H2, P])
    high = s.sb("high", [P, 2, H2, P], F32R)
    low = s.sb("low", [P, 2, H2, P], F32R)
    whigh = s.sb("whigh", [P, H2, RW * D], F32R)
    wlow = s.sb("wlow", [P, H2, RW * D], F32R)
    qe = s.sb("qe", [P, H2, P])
    qr = s.sb("qr", [P, H2, P])
    qf = s.sb("qf", [P, H2, P])
    den = s.sb("den", [P, H2, P])
    oT = s.sb("oT", [P, H2, P])
    xb = s.sb("xb", [P, 2, D])
    ob = s.sb("ob", [P, 2, D])
    pq = s.ps("pq", [P, H2, P])
    pnd = s.ps("pnd", [P, 2, H2, P])
    po = s.ps("po", [P, 512])
    dve_own = g.dve_own
    load, cut_ok, cut_free = s.sem("load"), s.sem("cut_ok"), s.sem("cut_free")
    high_ok, low_ok = s.sem("high_ok"), s.sem("low_ok")
    q_ok, q_free, qe_ok, qf_ok, nd_ok, oT_ok = (s.sem(n) for n in ("q_ok", "q_free", "qe_ok", "qf_ok", "nd_ok", "oT_ok"))
    o_ok, o_free, ob_ok, xb_free = (s.sem(n) for n in ("o_ok", "o_free", "ob_ok", "xb_free"))
    xb_in = [s.sem(f"xb_in{k}") for k in range(2)]
    ob_out = [s.sem(f"ob_out{k}") for k in range(2)]
    block = ctx.enter_context(nc.Block())

    @block.sync
    def _(eng):
        load_weights(eng, g, a, m.wr, 0, load)

        def load_x(b, k, rows=P):
            take(eng, xb_free)
            eng.dma_start(xb[0:rows, k, :], a["x"][ds(b * P, rows), :]).then_inc(xb_in[k], 16)

        def store(b, k):
            take(eng, ob_ok)
            eng.dma_start(g.base[ds(b * P, P), :], ob[:, k, :]).then_inc(ob_out[k], 16)

        eng.sem_inc(xb_free, 2)
        load_x(0, 0)
        load_x(1, 1)
        with eng.Fori(0, NB // 2 - 1) as i:
            for k in range(2):
                store(i * 2 + k, k)
                load_x(i * 2 + 2 + k, k)
        store(NB - 3, 0)
        load_x(NB - 1, 0, LAST)
        store(NB - 2, 1)
        store(NB - 1, 0)
        for k in range(2):
            eng.wait_ge(ob_out[k], 16)

    @block.gpsimd
    def _(eng):
        def step(b, k, prev):
            take(eng, cut_free)
            nc.gpsimd.tensor_copy(cut[:, k, :, :], g.xT[:, :, ds(b * P, P)]).then_inc(cut_ok, 1)

        eng.sem_inc(cut_free, 2)
        blocks_in_twos(eng, step)

    @block.tensor
    def _(eng):
        def project():
            take(eng, oT_ok)
            take(eng, o_free)
            for h in range(H2):
                mm = nc.tensor.matmul(po[:, 0:D], oT[:, h, :], wo[:, h, :], start=(h == 0), stop=(h == H2 - 1))
            mm.then_inc(o_ok, 1)

        def step(b, k, prev):
            take(eng, cut_ok)
            take(eng, q_free)
            for n in range(H2):
                for h in range(H2):
                    mm = nc.tensor.matmul(pq[:, n, :], wq[:, h, n * P:(n + 1) * P], cut[:, k, h, :],
                                          start=(h == 0), stop=(h == H2 - 1))
            mm.then_inc(q_ok, 1)
            take(eng, low_ok)
            x, w = (high[:, k, :, :], low[:, k, :, :]), (whigh, wlow)
            m.multiply_split(eng, x, w, 0, 2)
            if prev:
                project()
            m.multiply_split(eng, x, w, 2)
            take(eng, qf_ok)
            for n in range(H2):
                nc.tensor.matmul(pnd[:, 0, n, :], kvd[:, n, :], qf[:, n, :], start=True, stop=True)
                mm = nc.tensor.matmul(pnd[:, 1, n, :], ksd[:, n, :], qf[:, n, :], start=True, stop=True)
            mm.then_inc(nd_ok, 1)

        take(eng, low_ok)
        blocks_in_twos(eng, step)
        project()

    @block.scalar
    def _(eng):
        def high_part(b, k):
            nc.scalar.copy(high[:, k, :, :], g.xT[:, :, ds(b * P, P)]).then_inc(high_ok, 1)

        def step(b, k, prev, last):
            take(eng, q_ok)
            for n in range(H2):
                ins = nc.scalar.activation(qe[:, n, :], pq[:, n, :], ACT.Exp, bias=bq[:, n:n + 1])
            ins.then_inc(qe_ok, 1)
            if not last:
                high_part(b + 1, 1 - k)
            m.store(eng, b, k)
            eng.sem_inc(cut_free, 1)

        m.begin(eng)
        eng.wait_ge(load, 48)
        nc.scalar.copy(whigh[:, :, :], m.wr[:, :, :, :].rearrange("p h r o -> p h (r o)")).then_inc(high_ok, 1)
        high_part(0, 0)
        blocks_ahead(eng, step)
        m.end(eng)

    @block.vector
    def _(eng):
        def seq(ins):
            ins.then_inc(dve_own, 1)
            take(eng, dve_own)

        def finish(k):
            take(eng, xb_in[k], 16)
            take(eng, ob_out[k], 16)
            seq(nc.vector.tensor_tensor(ob[:, k, :], xb[:, k, :], bo[:, :], ALU.add))
            eng.sem_inc(xb_free, 1)
            take(eng, o_ok)
            seq(nc.vector.tensor_tensor(ob[:, k, :], ob[:, k, :], po[:, 0:D], ALU.add))
            eng.sem_inc(o_free, 1)
            eng.sem_inc(ob_ok, 1)

        def low_part(b, k):
            take(eng, high_ok)
            nc.vector.tensor_tensor(low[:, k, :, :], g.xT[:, :, ds(b * P, P)], high[:, k, :, :],
                                    ALU.subtract).then_inc(low_ok, 1)

        def step(b, k, prev, last):
            take(eng, qe_ok)
            for n in range(H2):
                ins = nc.vector.tensor_scalar(qr[:, n, :], pq[:, n, :], bq[:, n:n + 1], 0.0, ALU.add, ALU.max)
            seq(ins)
            eng.sem_inc(q_free, 1)
            seq(nc.vector.scalar_tensor_tensor(out=qf[:, :, :], in0=qe[:, :, :], scalar=1.0, in1=qr[:, :, :],
                                               op0=ALU.min, op1=ALU.add))
            eng.sem_inc(qf_ok, 1)
            if not last:
                low_part(b + 1, 1 - k)
            if prev:
                finish(1 - k)
            take(eng, nd_ok)
            seq(nc.vector.tensor_scalar(den[:, :, :], pnd[:, 1, :, :], 1e-6, None, ALU.add))
            seq(nc.vector.reciprocal(den[:, :, :], den[:, :, :]))
            seq(nc.vector.tensor_tensor(oT[:, :, :], pnd[:, 0, :, :], den[:, :, :], ALU.mult))
            eng.sem_inc(oT_ok, 1)

        eng.sem_inc(q_free, 1)
        eng.sem_inc(o_free, 1)
        for k in range(2):
            eng.sem_inc(ob_out[k], 16)
        take(eng, high_ok)
        nc.vector.tensor_tensor(wlow[:, :, :], m.wr[:, :, :, :].rearrange("p h r o -> p h (r o)"), whigh[:, :, :],
                                ALU.subtract).then_inc(low_ok, 1)
        low_part(0, 0)
        blocks_ahead(eng, step)
        finish((NB - 1) % 2)


class Aggregate:

    def __init__(self, nc, s, g, l):
        self.nc, self.g, self.l = nc, g, l
        self.ring = s.sb("ring", [P, RG, TPG, ROW])
        self.slot = s.sb("slot", [P, 2 * RG * TPG], I32)
        self.col = s.sb("col", [P, 2, P])
        self.oh = s.sb("oh", [P, TPG, P])
        self.pagg = s.ps("pagg", [P, 2, 512])
        sems = g.agg_sems
        self.pairs = s.sem("pairs")
        self.slot_ok, self.groups_in, self.gate, self.ring_ok = (sems[n] for n in ("slot_ok", "groups_in", "gate", "ring_ok"))
        self.landed = g.landed[l]
        self.agg_ok, self.agg_free = sems["agg_ok"], sems["agg_free"]
        self.oh_ok = [sems[f"oh_ok{t}"] for t in range(TPG)]
        self.oh_free = [sems[f"oh_free{t}"] for t in range(TPG)]

    def groups_of(self, eng, b):
        return (eng.value_load(self.g.bound[0:1, ds(b, 1)], min_val=0, max_val=NG - 1),
                eng.value_load(self.g.bound[0:1, ds(b + 1, 1)], min_val=0, max_val=NG - 1))

    def count(self, eng):
        def one(i, j):
            eng.wait_ge(self.landed[j], i * (16 * TPG) + 16 * TPG)
            eng.sem_inc(self.groups_in, 1)

        with eng.Fori(0, NG // RG) as i:
            for j in range(RG):
                one(i, j)
        for j in range(NG % RG):
            one(NG // RG, j)

    def gather(self, eng):
        def groups(i, half, wait=True, n=RG):
            to = half * RG * TPG
            self.nc.gpsimd.tensor_copy(self.slot[:, to:to + n * TPG],
                                       self.g.idx[:, ds(i * (RG * TPG), n * TPG)]).then_inc(self.slot_ok, 1)
            take(eng, self.slot_ok)
            for j in range(n):
                if wait:
                    last = eng.value_load(self.g.reuse[0:1, ds(i * RG + j - RG, 1)], min_val=1, max_val=NG + NB)
                    eng.wait_ge(self.pairs, last)
                    eng.sem_inc(self.gate, 1)
                for t in range(TPG):
                    at = to + j * TPG + t
                    eng.indirect_dma_start(self.ring[:, j, t, 0:D], None, self.g.table[self.l][:, :],
                                           bass.IndirectOffsetOnAxis(ap=self.slot[:, at:at + 1], axis=0)
                                           ).then_inc(self.landed[j], 16)

        full = NG // RG
        groups(0, 0, wait=False)
        with eng.Fori(0, (full - 1) // 2) as i:
            groups(i * 2 + 1, 1)
            groups(i * 2 + 2, 0)
        for i in range(1 + (full - 1) // 2 * 2, full):
            groups(i, i % 2)
        if NG % RG:
            groups(full, full % 2, n=NG % RG)

    def begin(self, eng):
        eng.sem_inc(self.agg_free, 2)
        for t in range(TPG):
            eng.sem_inc(self.oh_free[t], 1)
        for j in range(RG):
            ins = self.nc.vector.memset(self.ring[:, j, :, D:ROW], 1.0)
        ins.then_inc(self.ring_ok, 1)

    def end(self, eng):
        take(eng, self.agg_free, 2)
        for t in range(TPG):
            take(eng, self.oh_ok[t])

    def numbers(self, b, k, seq):
        g = self.g
        seq(self.nc.vector.tensor_scalar(self.col[:, k, :], g.iota[:, :], g.blockno[:, ds(b, 1)], None, ALU.add))

    def pair(self, eng, q, k):
        for t in range(TPG):
            take(eng, self.oh_free[t])
            self.nc.vector.tensor_scalar(self.oh[:, t, :].unsqueeze(1), self.col[:, ds(k, 1), :],
                                         self.g.dst[:, ds(q * TPG + t, 1)], None, ALU.is_equal).then_inc(self.oh_ok[t], 1)

    def first_pair(self, eng, seq):
        self.numbers(0, 0, seq)
        self.pair(eng, 0, 0)

    def onehots(self, eng, b, k, seq):
        q0, q1 = self.groups_of(eng, b)
        self.numbers(b + 1, 1 - k, seq)
        with eng.Fori(q0, q1 + 1) as q:
            more = ((q1 - q + 255) >> 8) & 1
            self.pair(eng, q + more, more * (2 * k - 1) + (1 - k))

    def sum(self, eng, b, k):
        nc, g, pagg = self.nc, self.g, self.pagg
        q0, q1 = self.groups_of(eng, b)
        take(eng, self.agg_free)
        nc.tensor.matmul(pagg[:, k, 0:2], g.zero[:, :], g.zero[:, 0:2], start=True, stop=False, skip_group_check=True)
        with eng.Fori(q0, q1 + 1) as q:
            eng.wait_ge(self.groups_in, q + 1)
            for t in range(TPG):
                take(eng, self.oh_ok[t])
                nc.tensor.matmul(pagg[:, k, 0:D + 1], self.oh[:, t, :],
                                 self.ring[:, ds(q & (RG - 1), 1), t, 0:D + 1].rearrange("p o n -> p (o n)"),
                                 start=False, stop=False, skip_group_check=True).then_inc(self.oh_free[t], 1)
            nc.tensor.matmul(pagg[:, k, 0:2], g.zero[:, :], g.zero[:, 0:2], start=False, stop=False,
                             skip_group_check=True).then_inc(self.pairs, 1)
        nc.tensor.matmul(pagg[:, k, 0:2], g.zero[:, :], g.zero[:, 0:2], start=False, stop=True,
                         skip_group_check=True).then_inc(self.agg_ok, 1)


def gnn_first(nc, g, a):
    with ExitStack() as ctx:
        s = Scope(nc, ctx, "gnn0")
        m = Messages(nc, s, g, 1)
        agg = Aggregate(nc, s, g, 0)
        own = s.sb("own", [P, 2, D])
        xn = s.sb("xn", [P, D])
        xT = s.sb("xT", [P, H2, P])
        dm = s.sb("dm", [P, 1])
        pT = s.ps("pT", [P, 512])
        load, xn_ok, xn_free = (s.sem(n) for n in ("load", "xn_ok", "xn_free"))
        dve_own, xT_ps, xT_ok, own_in = g.dve_own, g.xT_ps, g.xT_ok, g.moved
        block = ctx.enter_context(nc.Block())

        @block.sync
        def _(eng):
            load_weights(eng, g, a, m.wr, 1, load)
            agg.count(eng)

        @block.gpsimd
        def _(eng):
            agg.gather(eng)

        @block.vector
        def _(eng):
            def seq(ins):
                ins.then_inc(dve_own, 1)
                take(eng, dve_own)

            def step(b, k, prev):
                agg.onehots(eng, b, k, seq)
                take(eng, agg.agg_ok)
                seq(nc.vector.tensor_scalar(dm[:, :], agg.pagg[:, k, D:D + 1], 1.0, None, ALU.max))
                seq(nc.vector.reciprocal(g.dinv[:, ds(b, 1)], dm[:, :]))
                take(eng, xn_free)
                take(eng, own_in[k], 16)
                seq(nc.vector.scalar_tensor_tensor(out=xn[:, :], in0=agg.pagg[:, k, 0:D], scalar=g.dinv[:, ds(b, 1)],
                                                   in1=own[:, k, :], op0=ALU.mult, op1=ALU.add))
                eng.sem_inc(agg.agg_free, 1)
                seq(nc.vector.tensor_scalar(xn[:, :], xn[:, :], 0.0, None, ALU.max))
                eng.sem_inc(xn_ok, 1)

            eng.sem_inc(xn_free, 1)
            agg.begin(eng)
            agg.first_pair(eng, seq)
            blocks_in_twos(eng, step)
            agg.end(eng)

        @block.tensor
        def _(eng):
            def step(b, k, prev):
                agg.sum(eng, b, k)
                if prev:
                    take(eng, xT_ok)
                    m.multiply(eng, xT)
                take(eng, xn_ok)
                for h in range(H2):
                    mm = nc.tensor.transpose(pT[:, h * P:(h + 1) * P], xn[:, h * P:(h + 1) * P], g.ident[:, :])
                mm.then_inc(xT_ps, 1)

            take(eng, agg.ring_ok)
            eng.wait_ge(load, 48)
            blocks_in_twos(eng, step)
            take(eng, xT_ok)
            m.multiply(eng, xT)
            eng.sem_inc(agg.groups_in, -NG)

        @block.scalar
        def _(eng):
            def step(b, k, prev):
                rows = g.table[0][ds(b * (P * RW), P * RW), :].rearrange("(p r) d -> p r d", r=RW)
                eng.dma_start(own[:, k, :], rows[:, R, :]).then_inc(own_in[k], 16)
                if prev:
                    m.store(eng, b - 1, 1 - k)
                take(eng, xT_ps)
                eng.sem_inc(xn_free, 1)
                nc.scalar.copy(xT[:, :, :], pT[:, 0:D].rearrange("p (h n) -> p h n", h=H2)).then_inc(xT_ok, 1)

            m.begin(eng)
            blocks_in_twos(eng, step)
            m.store(eng, NB - 1, (NB - 1) % 2)
            m.end(eng)


def gnn_second(nc, g, a, r):
    with ExitStack() as ctx:
        s = Scope(nc, ctx, "gnn1")
        agg = Aggregate(nc, s, g, 1)
        own = s.sb("own", [P, 2, D])
        base = s.sb("base", [P, 2, D])
        sm = s.sb("sm", [P, D])
        xf = s.sb("xf", [P, 2, D])
        xfT = s.sb("xfT", [P, H2, P])
        rw = s.sb("rw", [P, H2, E])
        st = s.sb("st", [P, 12])
        eps = s.sb("eps", [P, 1])
        pT = s.ps("pT", [P, 512])
        pl = s.ps("pl", [P, 512])
        load, act_own = s.sem("load"), s.sem("act_own")
        dve_own, xT_ps, xfT_ok, own_in = g.dve_own, g.xT_ps, g.xT_ok, g.moved
        var_ok, std_ok, xf_ok, xf_free = (s.sem(n) for n in ("var_ok", "std_ok", "xf_ok", "xf_free"))
        xf_kept, lg_ok, lg_free = (s.sem(n) for n in ("xf_kept", "lg_ok", "lg_free"))
        base_in = [s.sem(f"base_in{k}") for k in range(2)]
        block = ctx.enter_context(nc.Block())

        @block.sync
        def _(eng):
            eng.dma_start(rw[:, :, :], a["L0_ffn_router_w"].rearrange("(h p) e -> p h e", p=P)).then_inc(load, 16)
            agg.count(eng)

        @block.gpsimd
        def _(eng):
            agg.gather(eng)

        @block.vector
        def _(eng):
            def seq(ins):
                ins.then_inc(dve_own, 1)
                take(eng, dve_own)

            def finish(b, k):
                x2 = r.x2[:, ds(b, 1), :].rearrange("p o d -> p (o d)")
                take(eng, agg.agg_ok)
                take(eng, own_in[k], 16)
                seq(nc.vector.scalar_tensor_tensor(out=sm[:, :], in0=agg.pagg[:, k, 0:D], scalar=g.dinv[:, ds(b, 1)],
                                                   in1=own[:, k, :], op0=ALU.mult, op1=ALU.add))
                eng.sem_inc(agg.agg_free, 1)
                take(eng, base_in[k], 16)
                seq(nc.vector.tensor_tensor(x2, sm[:, :], base[:, k, :], ALU.add))
                seq(nc.vector.bn_stats(st[:, 0:6], x2))
                nc.vector.bn_aggr(st[:, 6:8], st[:, 0:6]).then_inc(var_ok, 1)
                take(eng, std_ok)
                seq(nc.vector.reciprocal(st[:, 9:10], st[:, 8:9]))
                take(eng, xf_free, 2)
                seq(nc.vector.tensor_scalar(xf[:, k, :], x2, st[:, 6:7], st[:, 9:10], ALU.subtract, ALU.mult))
                eng.sem_inc(xf_ok, 1)
                eng.sem_inc(xf_kept, 1)

            def step(b, k, prev):
                agg.onehots(eng, b, k, seq)
                finish(b, k)

            eng.sem_inc(xf_free, 4)
            agg.begin(eng)
            seq(nc.vector.memset(eps[:, :], EPS))
            agg.first_pair(eng, seq)
            blocks_in_twos(eng, step)
            agg.end(eng)

        @block.tensor
        def _(eng):
            def logits(k):
                take(eng, xf_ok)
                for h in range(H2):
                    mm = nc.tensor.transpose(pT[:, h * P:(h + 1) * P], xf[:, k, h * P:(h + 1) * P], g.ident[:, :])
                mm.then_inc(xT_ps, 1)
                take(eng, xfT_ok)
                eng.sem_inc(xf_free, 1)
                take(eng, lg_free)
                for h in range(H2):
                    mm = nc.tensor.matmul(pl[:, 0:E], xfT[:, h, :], rw[:, h, :], start=(h == 0), stop=(h == H2 - 1))
                mm.then_inc(lg_ok, 1)

            def step(b, k, prev):
                agg.sum(eng, b, k)
                if prev:
                    logits(1 - k)

            take(eng, agg.ring_ok)
            eng.wait_ge(load, 16)
            blocks_in_twos(eng, step)
            logits((NB - 1) % 2)
            eng.sem_inc(agg.groups_in, -NG)

        @block.scalar
        def _(eng):
            def logits(b):
                take(eng, xT_ps)
                nc.scalar.copy(xfT[:, :, :], pT[:, 0:D].rearrange("p (h n) -> p h n", h=H2)).then_inc(xfT_ok, 1)
                take(eng, lg_ok)
                nc.scalar.copy(r.lg[:, ds(b * E, E)], pl[:, 0:E]).then_inc(lg_free, 1)

            def step(b, k, prev):
                rows = g.table[1][ds(b * (P * RW), P * RW), :].rearrange("(p r) d -> p r d", r=RW)
                eng.dma_start(own[:, k, :], rows[:, R, :]).then_inc(own_in[k], 16)
                eng.dma_start(base[:, k, :], g.base[ds(b * P, P), :]).then_inc(base_in[k], 16)
                if prev:
                    logits(b - 1)
                take(eng, var_ok)
                nc.scalar.activation(st[:, 8:9], st[:, 7:8], ACT.Sqrt, bias=eps[:, :]).then_inc(std_ok, 1)
                take(eng, xf_kept)
                nc.scalar.copy(r.xf[:, ds(b, 1), :].rearrange("p o d -> p (o d)"), xf[:, k, :]).then_inc(act_own, 1)
                take(eng, act_own)
                eng.sem_inc(xf_free, 1)

            eng.sem_inc(lg_free, 1)
            blocks_in_twos(eng, step)
            logits(NB - 1)


class Routed:

    def __init__(self, s, g):
        self.x2 = s.sb("x2", [P, NB, D])
        self.xf = g.xT[:, :, :].rearrange("p h n -> p (h n)").rearrange("p (b d) -> p b d", d=D)
        self.lg = s.sb("lg", [P, NB * E])


def experts(nc, g, a, r, out):
    NTL = MAXT + TU
    NR = 7
    with ExitStack() as ctx:
        s = Scope(nc, ctx, "exp")
        w1 = s.sb("w1", [P, E, H2 * HID + 1])
        b1 = s.sb("b1", [HID, E])
        w2 = s.sb("w2", [HID + 1, E, D])
        tri = s.sb("tri", [P, P], BF16)
        one = s.sb("one", [P, P], BF16)
        cnt = s.sb("cnt", [P, 4, E])
        cnti = s.sb("cnti", [P, 2, E], I32)
        pos = s.sb("pos", [P, NB])
        posi = s.sb("posi", [P, NB], I32)
        te = s.sb("te", [1, NTL])
        tei = s.sb("tei", [1, NTL], I32)
        rounds = s.sb("rounds", [1, 1], I32)
        rdf = s.sb("rdf", [1, 1])
        xb = s.sb("xb", [P, TU, D])
        xbT = s.sb("xbT", [P, 2, H2, P])
        ws = s.sb("ws", [P, TU, H2 * HID + 1])
        hT = s.sb("hT", [HID + 1, 2, P])
        yb = s.sb("yb", [P, 2, D])

        one_ok, w_in, oh_ok, rank_ps, cnt_ps, pos_ok = (s.sem(n) for n in (
            "one_ok", "w_in", "oh_ok", "rank_ps", "cnt_ps", "pos_ok"))
        rb_in = g.moved[0]
        dve_own, xT_ps, xT_ok = g.dve_own, g.xT_ps, g.xT_ok
        scattered, landed = g.scattered, g.landed_back
        xb_free = s.sem("xb_free")
        ws_ok, ws_free, h_ps, h_ok, hT_free, y_ps, y_done, y_free, y_ok = (s.sem(n) for n in (
            "ws_ok", "ws_free", "h_ps", "h_ok", "hT_free", "y_ps", "y_done", "y_free", "y_ok"))
        xb_in = [s.sem(f"xb_in{k}") for k in range(TU)]
        yb_out = [s.sem(f"yb_out{k}") for k in range(2)]
        yg_in, yg_free, ob_ok = s.sem("yg_in"), s.sem("yg_free"), s.sem("ob_ok")
        ob_out = [s.sem(f"ob_out{k}") for k in range(NR)]

        with ExitStack() as c1:
            s1 = Scope(nc, c1, "exp1")
            less = s1.sb("less", [P, E, E])
            rank = s1.sb("rank", [P, NB * E])
            tl = s1.sb("tl", [1, NTL, E])
            rb = s1.sb("rb", [P, E])
            mx = s1.sb("mx", [P, NB])
            oh = s1.sb("oh", [P, NB * E], BF16)
            acc = s1.sb("acc", [P, (NB + 1) * E], BF16)
            pr = s1.ps("pr", [P, 4, 512])
            pc = s1.ps("pc", [P, 512])
            block = c1.enter_context(nc.Block())
            cuts = [(lo, min(lo + 512, NB * E)) for lo in range(0, NB * E, 512)]

            @block.sync
            def _(eng):
                eng.dma_start(rb[:, :], a["L0_ffn_router_b"].rearrange("(o d) -> o d", o=1).to_broadcast([P, E])).then_inc(rb_in, 16)
                for h in range(H2):
                    eng.dma_start(w1[:, :, h * HID:(h + 1) * HID],
                                  a["L0_ffn_W1"][:, h * P:(h + 1) * P, :].rearrange("e p n -> p e n")).then_inc(w_in, 16)
                eng.dma_start(b1[:, :], a["L0_ffn_b1"]).then_inc(w_in, 16)
                eng.dma_start(w2[0:HID, :, :], a["L0_ffn_W2"].rearrange("e n d -> n e d")).then_inc(w_in, 16)
                eng.dma_start(w2[HID:HID + 1, :, :], a["L0_ffn_b2"].rearrange("(o e) d -> o e d", o=1)).then_inc(w_in, 16)

            @block.gpsimd
            def _(eng):
                nc.gpsimd.memset(one[:, :], 1.0).then_inc(one_ok, 1)
                eng.wait_ge(one_ok, 1)
                nc.gpsimd.affine_select(out=tri[:, :], in_=one[:, :], compare_op=ALU.is_gt, fill=0.0, base=0,
                                        pattern=[[1, P]], channel_multiplier=-1).then_inc(one_ok, 1)
                eng.wait_ge(pos_ok, 1)
                for b in range(NB):
                    eng.indirect_dma_start(g.bucket[:, :], bass.IndirectOffsetOnAxis(ap=posi[:, b:b + 1], axis=0),
                                           r.xf[:, b, :], None).then_inc(scattered, 16)
                eng.wait_ge(scattered, 16 * NB)

            @block.tensor
            def _(eng):
                eng.wait_ge(one_ok, 2)
                eng.wait_ge(oh_ok, 1)
                nc.tensor.matmul(pc[:, 0:E], one[:, :], acc[:, NB * E:(NB + 1) * E], start=True, stop=True).then_inc(cnt_ps, 1)
                for n, (lo, hi) in enumerate(cuts):
                    nc.tensor.matmul(pr[:, n, 0:hi - lo], tri[:, :], oh[:, lo:hi], start=True, stop=False)
                    mm = nc.tensor.matmul(pr[:, n, 0:hi - lo], one[:, :], acc[:, lo:hi], start=False, stop=True)
                mm.then_inc(rank_ps, 1)

            @block.vector
            def _(eng):
                def seq(ins):
                    ins.then_inc(dve_own, 1)
                    take(eng, dve_own)

                nc.vector.memset(w1[HID:P, :, H2 * HID:], 0.0)
                nc.vector.memset(hT[HID:HID + 1, :, :], 1.0)
                row = g.iota[:, 0:E]
                seq(nc.vector.tensor_tensor(less[:, :, :], row.unsqueeze(1).to_broadcast([P, E, E]),
                                            row.unsqueeze(2).to_broadcast([P, E, E]), ALU.is_lt))
                lg = r.lg[:, :].rearrange("p (b e) -> p b e", e=E)
                most = mx[:, :].unsqueeze(2).to_broadcast([P, NB, E])
                eng.wait_ge(rb_in, 16)
                seq(nc.vector.tensor_tensor(lg, lg, rb[:, :].unsqueeze(1).to_broadcast([P, NB, E]), ALU.add))
                seq(nc.vector.tensor_reduce(mx[:, :], lg, AX.X, ALU.max))
                seq(nc.vector.tensor_tensor(lg, lg, most, ALU.is_equal))
                seq(nc.vector.scalar_tensor_tensor(out=lg, in0=lg, scalar=-2.0 * E,
                                                   in1=row.unsqueeze(1).to_broadcast([P, NB, E]), op0=ALU.mult, op1=ALU.add))
                seq(nc.vector.tensor_reduce(mx[:, :], lg, AX.X, ALU.min))
                seq(nc.vector.tensor_tensor(oh[:, :].rearrange("p (b e) -> p b e", e=E), lg, most, ALU.is_equal))
                seq(nc.vector.memset(acc[:, 0:E], 0.0))
                for b in range(NB):
                    seq(nc.vector.tensor_tensor(acc[:, (b + 1) * E:(b + 2) * E], acc[:, b * E:(b + 1) * E],
                                                oh[:, b * E:(b + 1) * E], ALU.add))
                eng.sem_inc(oh_ok, 1)
                take(eng, cnt_ps)
                seq(nc.vector.tensor_scalar(cnt[:, 0, :], pc[:, 0:E], float(P - 1), None, ALU.add))
                seq(nc.vector.tensor_copy(cnti[:, 0, :], cnt[:, 0, :]))
                seq(nc.vector.tensor_scalar(cnti[:, 1, :], cnti[:, 0, :], 7, None, ALU.logical_shift_right))
                seq(nc.vector.tensor_copy(cnt[:, 1, :], cnti[:, 1, :]))
                seq(nc.vector.tensor_tensor(less[:, :, :], less[:, :, :], cnt[:, 1, :].unsqueeze(1).to_broadcast([P, E, E]),
                                            ALU.mult))
                seq(nc.vector.tensor_reduce(cnt[:, 2, :], less[:, :, :], AX.X, ALU.add))
                seq(nc.vector.tensor_scalar(cnt[:, 3, :], cnt[:, 2, :], float(P), None, ALU.mult))
                take(eng, rank_ps)
                for n, (lo, hi) in enumerate(cuts):
                    w = (hi - lo) // E
                    ins = nc.vector.tensor_tensor(rank[:, lo:hi].rearrange("p (b e) -> p b e", e=E),
                                                  pr[:, n, 0:hi - lo].rearrange("p (b e) -> p b e", e=E),
                                                  cnt[:, 3, :].unsqueeze(1).to_broadcast([P, w, E]), ALU.add)
                seq(ins)
                seq(nc.vector.tensor_tensor(rank[:, :], rank[:, :], oh[:, :], ALU.mult))
                seq(nc.vector.tensor_reduce(pos[:, :], rank[:, :].rearrange("p (b e) -> p b e", e=E), AX.X, ALU.add))
                nc.vector.tensor_copy(posi[:, :], pos[:, :]).then_inc(pos_ok, 1)
                seq(nc.vector.tensor_tensor(cnt[:, 0, :], cnt[:, 1, :], cnt[:, 2, :], ALU.add))
                seq(nc.vector.tensor_tensor(tl[:, :, :], cnt[0:1, 0, :].unsqueeze(1).to_broadcast([1, NTL, E]),
                                            g.iota[0:1, 0:NTL].unsqueeze(2).to_broadcast([1, NTL, E]), ALU.is_le))
                seq(nc.vector.tensor_reduce(te[:, :], tl[:, :, :], AX.X, ALU.add))
                seq(nc.vector.tensor_scalar(tei[:, :], te[:, :], float(E - 1), None, ALU.min))
                seq(nc.vector.tensor_scalar(rdf[:, :], cnt[0:1, 0, E - 1:E], float(TU - 1), None, ALU.add))
                seq(nc.vector.tensor_copy(rounds[:, :], rdf[:, :]))
                seq(nc.vector.tensor_scalar(rounds[:, :], rounds[:, :], 2, None, ALU.logical_shift_right))
                eng.wait_ge(w_in, 80)
                nc.vector.tensor_copy(w1[0:HID, :, H2 * HID:], b1[:, :].unsqueeze(2))

        with ExitStack() as c2:
            s2 = Scope(nc, c2, "exp2")
            pT = s2.ps("pT", [P, 2, 512])
            ph = s2.ps("ph", [HID, 2, 512])
            py = s2.ps("py", [P, 2, 512])
            block = c2.enter_context(nc.Block())

            def stages(eng, ahead, middle, back):
                n = eng.value_load(rounds[0:1, 0:1], min_val=1, max_val=MAXT // TU)
                ahead(0, 0)
                ahead(1, 1)
                middle(0, 0)
                with eng.Fori(0, n) as i:
                    for u in range(TU):
                        ahead(i * TU + u + 2, (u + 2) % TU)
                        middle(i * TU + u + 1, (u + 1) % TU)
                        back(i * TU + u, u)

            def nothing(t, u):
                pass

            def expert(eng, t):
                return eng.value_load(tei[0:1, ds(t, 1)], min_val=0, max_val=E - 1)

            @block.sync
            def _(eng):
                def load(t, u):
                    take(eng, xb_free)
                    eng.dma_start(xb[:, u, :], g.bucket[ds(t * P, P), :]).then_inc(xb_in[u], 16)

                n = eng.value_load(rounds[0:1, 0:1], min_val=1, max_val=MAXT // TU)
                eng.sem_inc(xb_free, TU)
                for u in range(TU):
                    load(u, u)
                with eng.Fori(0, n) as i:
                    for u in range(TU):
                        load(i * TU + u + TU, u)
                        take(eng, y_ok)
                        eng.dma_start(g.routed[ds((i * TU + u) * P, P), :], yb[:, u % 2, :]).then_inc(yb_out[u % 2], 16)
                for u in range(2, TU):
                    eng.wait_ge(xb_in[u], 16)

            @block.gpsimd
            def _(eng):
                def weights(t, u):
                    e = expert(eng, t)
                    take(eng, ws_free)
                    nc.gpsimd.tensor_copy(ws[:, u, :].unsqueeze(1), w1[:, ds(e, 1), :]).then_inc(ws_ok, 1)

                eng.sem_inc(ws_free, TU)
                stages(eng, nothing, weights, nothing)

            @block.tensor
            def _(eng):
                def ahead(t, u):
                    take(eng, xb_in[u], 16)
                    for h in range(H2):
                        mm = nc.tensor.transpose(pT[:, u % 2, h * P:(h + 1) * P], xb[:, u, h * P:(h + 1) * P], g.ident[:, :])
                    mm.then_inc(xT_ps, 1)

                def middle(t, u):
                    k = u % 2
                    take(eng, ws_ok)
                    take(eng, xT_ok)
                    for h in range(H2):
                        mm = nc.tensor.matmul(ph[:, k, 0:P], ws[:, u, h * HID:(h + 1) * HID], xbT[:, k, h, :],
                                              start=(h == 0), stop=(h == H2 - 1))
                    mm.then_inc(h_ps, 1)

                def back(t, u):
                    k = u % 2
                    e = expert(eng, t)
                    take(eng, h_ok)
                    eng.sem_inc(ws_free, 1)
                    take(eng, y_free)
                    nc.tensor.matmul(py[:, k, 0:D], hT[:, k, :], w2[:, ds(e, 1), :].rearrange("p o d -> p (o d)"),
                                     start=True, stop=True).then_inc(y_ps, 1)

                stages(eng, ahead, middle, back)

            @block.scalar
            def _(eng):
                def ahead(t, u):
                    take(eng, xT_ps)
                    eng.sem_inc(xb_free, 1)
                    nc.scalar.copy(xbT[:, u % 2, :, :], pT[:, u % 2, 0:D].rearrange("p (h n) -> p h n", h=H2)).then_inc(xT_ok, 1)

                def middle(t, u):
                    take(eng, h_ps)
                    take(eng, hT_free)
                    k = u % 2
                    nc.scalar.activation(hT[0:HID, k, :], ph[:, k, 0:P], ACT.Relu,
                                         bias=ws[0:HID, u, H2 * HID:]).then_inc(h_ok, 1)

                stages(eng, ahead, middle, nothing)

            @block.vector
            def _(eng):
                def back(t, u):
                    take(eng, y_ps)
                    eng.sem_inc(hT_free, 1)
                    take(eng, yb_out[u % 2], 16)
                    nc.vector.tensor_scalar(yb[:, u % 2, :], py[:, u % 2, 0:D], 0.0, None, ALU.max).then_inc(y_done, 1)
                    take(eng, y_done)
                    eng.sem_inc(y_free, 1)
                    eng.sem_inc(y_ok, 1)

                eng.sem_inc(hT_free, 2)
                eng.sem_inc(y_free, 2)
                for k in range(2):
                    eng.sem_inc(yb_out[k], 16)
                stages(eng, nothing, nothing, back)
                for k in range(2):
                    eng.wait_ge(yb_out[k], 16)

        with ExitStack() as c3:
            s3 = Scope(nc, c3, "exp3")
            yg = s3.sb("yg", [P, NR, D])
            ob = s3.sb("ob", [P, NR, D])
            block = c3.enter_context(nc.Block())

            @block.sync
            def _(eng):
                with eng.Fori(0, NB // NR) as i:
                    for j in range(NR):
                        eng.wait_ge(landed[j], i * 16 + 16)
                        eng.sem_inc(yg_in, 1)

            @block.gpsimd
            def _(eng):
                for b in range(NB):
                    if b >= NR:
                        take(eng, yg_free)
                    eng.indirect_dma_start(yg[:, b % NR, :], None, g.routed[:, :],
                                           bass.IndirectOffsetOnAxis(ap=posi[:, b:b + 1], axis=0)
                                           ).then_inc(landed[b % NR], 16)

            @block.vector
            def _(eng):
                for j in range(NR):
                    eng.sem_inc(ob_out[j], 16)
                with eng.Fori(0, NB // NR) as i:
                    for j in range(NR):
                        take(eng, yg_in)
                        take(eng, ob_out[j], 16)
                        nc.vector.tensor_tensor(ob[:, j, :].unsqueeze(1), yg[:, j, :].unsqueeze(1), r.x2[:, ds(i * NR + j, 1), :],
                                                ALU.add).then_inc(ob_ok, 1)

            @block.scalar
            def _(eng):
                def store(b, j, rows=P):
                    take(eng, ob_ok)
                    eng.sem_inc(yg_free, 1)
                    eng.dma_start(out[ds(b * P, rows), :], ob[0:rows, j, :]).then_inc(ob_out[j], 16)

                with eng.Fori(0, NB // NR - 1) as i:
                    for j in range(NR):
                        store(i * NR + j, j)
                for j in range(NR):
                    b = NB - NR + j
                    store(b, j, LAST if b == NB - 1 else P)
                for j in range(NR):
                    eng.wait_ge(ob_out[j], 16)


def program(nc, a, out):
    with ExitStack() as ctx:
        g = Shared(nc, ctx)
        prepare(nc, g, a)
        attention(nc, g, a)
        gnn_first(nc, g, a)
        r = Routed(Scope(nc, ctx, "rt"), g)
        gnn_second(nc, g, a, r)
        experts(nc, g, a, r, out)


def by_partition(edges, fill):
    padded = np.full((NTP * P,), fill, edges.dtype)
    padded[:NE] = edges
    return np.ascontiguousarray(padded.reshape(NTP, P).T)


def kernel(**inputs):
    import concourse.bacc as bacc
    from concourse.bass_utils import run_bass_kernel_spmd

    layout = dict(inputs)
    layout["src"] = by_partition(np.asarray(inputs["src"]), 0)
    layout["dst"] = by_partition(np.asarray(inputs["dst"]), PAD_DST)
    layout["edge_type_8"] = by_partition(np.asarray(inputs["edge_type_8"]), 0)
    layout["L0_gnn_coeffs"] = np.asarray(inputs["L0_gnn_coeffs"]).transpose(0, 2, 1)
    layout["L0_mix_bq"] = np.asarray(inputs["L0_mix_bq"]).reshape(H2, P).T
    layout["L0_ffn_router_w"] = np.asarray(inputs["L0_ffn_router_w"]).T
    layout["L0_ffn_b1"] = np.asarray(inputs["L0_ffn_b1"]).T

    nc = bacc.Bacc("TRN2", target_bir_lowering=False, num_devices=1)
    arrays, a = {}, {}
    for name, value in layout.items():
        value = np.ascontiguousarray(value)
        arrays[f"in_{name}"] = value
        a[name] = nc.dram_tensor(f"in_{name}", value.shape, mybir.dt.from_np(value.dtype), kind="ExternalInput").ap()
    out = nc.dram_tensor("out", (N, D), F32, kind="ExternalOutput").ap()
    program(nc, a, out)
    result = run_bass_kernel_spmd(nc, [arrays], core_ids=[0])
    return result.results[0]["out"]
```
